# Optimizing a Trainium2 kernel written in Bass

```python
import numpy as np
import jax
import jax.numpy as jnp

def _softmax(x, axis=-1):
    return jax.nn.softmax(x, axis=axis)

def _gelu(x):
    return jax.nn.gelu(x, approximate=True)

def _silu(x):
    return jax.nn.silu(x)

def _sigmoid(x):
    return jax.nn.sigmoid(x)

def _layernorm(x, axis=-1, eps=1e-05):
    m = jnp.mean(x, axis=axis, keepdims=True)
    v = jnp.var(x, axis=axis, keepdims=True)
    return (x - m) / jnp.sqrt(v + eps)

def _scatter_add(tgt, idx, src, axis=0):
    return tgt.at[idx].add(src)

def _segment_sum(src, seg, n):
    return jax.ops.segment_sum(src, seg, n)
kernel_name = 'mk_gnn_ffn_d2_gnn_r8_587a0b'

def setup_inputs(seed: int=0):
    np.random.seed(seed)
    _w = jnp.asarray

    def _rec_inputs():
        import jax
        import jax.numpy as jnp
        _gk = jax.random.key(seed)
        x = -0.0003713 + 1 * jax.random.normal(jax.random.fold_in(_gk, 1), (6250, 256), jnp.float32)
        src = jax.random.randint(jax.random.fold_in(_gk, 2), (200000,), 0, 6250, jnp.int32)
        dst = jax.random.randint(jax.random.fold_in(_gk, 3), (200000,), 0, 6250, jnp.int32)
        _o = jnp.argsort(dst, stable=True)
        src = src[_o]
        dst = dst[_o]
        edge_weight = -7.32377e-05 + 0.176746 * jax.random.normal(jax.random.fold_in(_gk, 13), (200000,), jnp.float32)
        return (x, src, dst, edge_weight)
    x, src, dst, edge_weight = _rec_inputs()

    def _L0_gnn_setup():
        import jax, jax.numpy as jnp
        import numpy as np
        N_NODES = 6250
        NNZ = 200000
        D_FEAT = 256
        key = jax.random.key(seed)
        k_x, k_v, k_r, k_c = jax.random.split(key, 4)
        x = jax.random.normal(k_x, (N_NODES, D_FEAT), dtype=jnp.float32)
        std = 1.0 / np.sqrt(NNZ / N_NODES)
        values = jax.random.normal(k_v, (NNZ,), dtype=jnp.float32) * std
        row = jax.random.randint(k_r, (NNZ,), 0, N_NODES, dtype=jnp.int64)
        col = jax.random.randint(k_c, (NNZ,), 0, N_NODES, dtype=jnp.int64)
        return {'x': x, 'values': values, 'row': row, 'col': col}
    _L0_gnn_all = _L0_gnn_setup()
    _L0_gnn_in = {k: v for k, v in _L0_gnn_all.items() if k in ()}
    del _L0_gnn_all

    def _L0_ffn_setup():
        import math
        import jax, jax.numpy as jnp
        import numpy as np
        CAPACITY_FACTOR = 1.25
        TOP_K = 2
        LN_EPS = 1e-05

        def _layer_norm(x, gamma, beta):
            mu = jnp.mean(x, axis=-1, keepdims=True)
            var = jnp.var(x, axis=-1, keepdims=True)
            return (x - mu) * jax.lax.rsqrt(var + LN_EPS) * gamma + beta
        key = jax.random.key(seed)
        ks = jax.random.split(key, 4)
        B, S, D, F, E = (8, 512, 256, 512, 8)
        x = jax.random.normal(ks[0], (B, S, D), dtype=jnp.float32)
        Wr = jax.random.normal(ks[1], (D, E), dtype=jnp.float32) / np.sqrt(D)
        br = jnp.zeros((E,), jnp.float32)
        W1 = jax.random.normal(ks[2], (E, D, F), dtype=jnp.float32) / np.sqrt(D)
        b1 = jnp.zeros((E, F), jnp.float32)
        W2 = jax.random.normal(ks[3], (E, F, D), dtype=jnp.float32) / np.sqrt(F)
        b2 = jnp.zeros((E, D), jnp.float32)
        gamma = jnp.ones((D,), jnp.float32)
        beta = jnp.zeros((D,), jnp.float32)
        return {'x': x, 'Wr': Wr, 'br': br, 'W1': W1, 'b1': b1, 'W2': W2, 'b2': b2, 'gamma': gamma, 'beta': beta}
    _L0_ffn_all = _L0_ffn_setup()
    _L0_ffn_in = {k: v for k, v in _L0_ffn_all.items() if k in ('Wr', 'br', 'W1', 'b1', 'W2', 'b2', 'gamma', 'beta')}
    del _L0_ffn_all

    def _L1_gnn_setup():
        import jax, jax.numpy as jnp
        import numpy as np
        N, IN_DIM, OUT_DIM, HEADS, E = (6250, 256, 256, 4, 100000)
        HEAD_DIM = OUT_DIM // HEADS
        NEG_SLOPE = 0.2
        key = jax.random.key(seed)
        k = jax.random.split(key, 6)
        h = jax.random.normal(k[0], (N, IN_DIM), dtype=jnp.float32)
        edge_index = jax.random.randint(k[1], (2, E), 0, N, dtype=jnp.int32)
        W = jax.random.normal(k[2], (OUT_DIM, IN_DIM), dtype=jnp.float32) * (1.0 / np.sqrt(IN_DIM))
        b = jnp.zeros((OUT_DIM,), dtype=jnp.float32)
        a_src = jax.random.normal(k[3], (HEADS, HEAD_DIM), dtype=jnp.float32) * (1.0 / np.sqrt(HEAD_DIM))
        a_dst = jax.random.normal(k[4], (HEADS, HEAD_DIM), dtype=jnp.float32) * (1.0 / np.sqrt(HEAD_DIM))
        return {'h': h, 'edge_index': edge_index, 'W': W, 'b': b, 'a_src': a_src, 'a_dst': a_dst}
    _L1_gnn_all = _L1_gnn_setup()
    _L1_gnn_in = {k: v for k, v in _L1_gnn_all.items() if k in ('W', 'b', 'a_src', 'a_dst')}
    del _L1_gnn_all

    def _L1_ffn_setup():
        import jax, jax.numpy as jnp
        import numpy as np
        B, T, D, H, L = (16, 512, 256, 256, 2)

        def _lstm(x, W_ih, W_hh, b_ih, b_hh):
            x_proj = jnp.einsum('btd,gd->btg', x, W_ih) + b_ih + b_hh
            h0 = jnp.zeros((x.shape[0], W_hh.shape[1]), x.dtype)
            c0 = jnp.zeros_like(h0)

            def step(carry, xp):
                h, c = carry
                gates = xp + h @ W_hh.T
                i, f, g, o = jnp.split(gates, 4, axis=-1)
                c = jax.nn.sigmoid(f) * c + jax.nn.sigmoid(i) * jnp.tanh(g)
                h = jax.nn.sigmoid(o) * jnp.tanh(c)
                return ((h, c), h)
            _, hs = jax.lax.scan(step, (h0, c0), jnp.swapaxes(x_proj, 0, 1))
            return jnp.swapaxes(hs, 0, 1)
        key = jax.random.key(seed)
        ks = jax.random.split(key, 9)
        s = 1.0 / np.sqrt(H)
        u = lambda k, shape: jax.random.uniform(k, shape, jnp.float32, -s, s)
        return {'x': jax.random.normal(ks[0], (B, T, D), jnp.float32), 'W_ih': u(ks[1], (4 * H, D)), 'W_hh': u(ks[2], (4 * H, H)), 'b_ih': u(ks[3], (4 * H,)), 'b_hh': u(ks[4], (4 * H,)), 'W_lin': u(ks[5], (L, H)), 'b_lin': u(ks[6], (L,)), 'fw_att': jnp.full((1, H), 0.001, jnp.float32), 'bw_att': jnp.full((1, H), 0.001, jnp.float32)}
    _L1_ffn_all = _L1_ffn_setup()
    _L1_ffn_in = {k: v for k, v in _L1_ffn_all.items() if k in ('W_ih', 'W_hh', 'b_ih', 'b_hh', 'W_lin', 'b_lin', 'fw_att', 'bw_att')}
    del _L1_ffn_all
    return {'x': x, 'src': src, 'dst': dst, 'edge_weight': edge_weight, 'L0_ffn_Wr': _L0_ffn_in['Wr'], 'L0_ffn_br': _L0_ffn_in['br'], 'L0_ffn_W1': _L0_ffn_in['W1'], 'L0_ffn_b1': _L0_ffn_in['b1'], 'L0_ffn_W2': _L0_ffn_in['W2'], 'L0_ffn_b2': _L0_ffn_in['b2'], 'L0_ffn_gamma': _L0_ffn_in['gamma'], 'L0_ffn_beta': _L0_ffn_in['beta'], 'L1_gnn_W': _L1_gnn_in['W'], 'L1_gnn_b': _L1_gnn_in['b'], 'L1_gnn_a_src': _L1_gnn_in['a_src'], 'L1_gnn_a_dst': _L1_gnn_in['a_dst'], 'L1_ffn_W_ih': _L1_ffn_in['W_ih'], 'L1_ffn_W_hh': _L1_ffn_in['W_hh'], 'L1_ffn_b_ih': _L1_ffn_in['b_ih'], 'L1_ffn_b_hh': _L1_ffn_in['b_hh'], 'L1_ffn_W_lin': _L1_ffn_in['W_lin'], 'L1_ffn_b_lin': _L1_ffn_in['b_lin'], 'L1_ffn_fw_att': _L1_ffn_in['fw_att'], 'L1_ffn_bw_att': _L1_ffn_in['bw_att']}

def reference(x, src, dst, edge_weight, L0_ffn_Wr, L0_ffn_br, L0_ffn_W1, L0_ffn_b1, L0_ffn_W2, L0_ffn_b2, L0_ffn_gamma, L0_ffn_beta, L1_gnn_W, L1_gnn_b, L1_gnn_a_src, L1_gnn_a_dst, L1_ffn_W_ih, L1_ffn_W_hh, L1_ffn_b_ih, L1_ffn_b_hh, L1_ffn_W_lin, L1_ffn_b_lin, L1_ffn_fw_att, L1_ffn_bw_att):
    import jax
    import jax.numpy as jnp

    def _L0_gnn_ref(x, values, row, col):
        import jax, jax.numpy as jnp
        import numpy as np
        N_NODES = 6250
        NNZ = 200000
        D_FEAT = 256
        msgs = values[:, None] * x[col]
        out = jax.ops.segment_sum(msgs, row, num_segments=N_NODES)
        return out

    def _L0_ffn_ref(x, Wr, br, W1, b1, W2, b2, gamma, beta):
        import math
        import jax, jax.numpy as jnp
        import numpy as np
        CAPACITY_FACTOR = 1.25
        TOP_K = 2
        LN_EPS = 1e-05

        def _layer_norm(x, gamma, beta):
            mu = jnp.mean(x, axis=-1, keepdims=True)
            var = jnp.var(x, axis=-1, keepdims=True)
            return (x - mu) * jax.lax.rsqrt(var + LN_EPS) * gamma + beta
        B, S, D = x.shape
        E = Wr.shape[1]
        N = B * S
        K = TOP_K
        logits = jnp.mean(x, axis=1) @ Wr + br
        routing_weights = jax.nn.softmax(logits, axis=-1)
        capacity = float(math.ceil(N * CAPACITY_FACTOR / E))
        expected_loads = routing_weights.sum(axis=0) * (N / B)
        scale = jnp.where(expected_loads > capacity, capacity / expected_loads, 1.0)
        routing_weights = jax.nn.softmax(routing_weights * scale, axis=-1)
        rw_tok = jnp.broadcast_to(routing_weights[:, None, :], (B, S, E)).reshape(N, E)
        top_w, top_i = jax.lax.top_k(rw_tok, K)
        top_w = jax.nn.softmax(top_w, axis=-1)
        xf = x.reshape(N, D)
        h = jax.nn.gelu(jnp.einsum('nd,edf->enf', xf, W1) + b1[:, None, :], approximate=False)
        y = jnp.einsum('enf,efd->end', h, W2) + b2[:, None, :]
        w_dense = jnp.zeros((N, E), x.dtype).at[jnp.arange(N)[:, None], top_i].add(top_w)
        out = jnp.einsum('ne,end->nd', w_dense, y).reshape(B, S, D)
        out = _layer_norm(out + x, gamma, beta)
        return out

    def _L1_gnn_ref(h, edge_index, W, b, a_src, a_dst):
        import jax, jax.numpy as jnp
        import numpy as np
        N, IN_DIM, OUT_DIM, HEADS, E = (6250, 256, 256, 4, 100000)
        HEAD_DIM = OUT_DIM // HEADS
        NEG_SLOPE = 0.2
        idx_i, idx_j = (edge_index[0], edge_index[1])
        Wh = (h @ W.T + b).reshape(N, HEADS, HEAD_DIM)
        alpha_src = jnp.einsum('nhd,hd->nh', Wh, a_src)
        alpha_dst = jnp.einsum('nhd,hd->nh', Wh, a_dst)
        e = jax.nn.leaky_relu(alpha_src[idx_i] + alpha_dst[idx_j], NEG_SLOPE)
        m = jax.ops.segment_max(e, idx_i, num_segments=N)
        ex = jnp.exp(e - m[idx_i])
        denom = jax.ops.segment_sum(ex, idx_i, num_segments=N)
        att = ex / denom[idx_i]
        out = jax.ops.segment_sum(att[:, :, None] * Wh[idx_j], idx_i, num_segments=N)
        return out.reshape(N, OUT_DIM)

    def _L1_ffn_ref(x, W_ih, W_hh, b_ih, b_hh, W_lin, b_lin, fw_att, bw_att):
        import jax, jax.numpy as jnp
        import numpy as np
        B, T, D, H, L = (16, 512, 256, 256, 2)

        def _lstm(x, W_ih, W_hh, b_ih, b_hh):
            x_proj = jnp.einsum('btd,gd->btg', x, W_ih) + b_ih + b_hh
            h0 = jnp.zeros((x.shape[0], W_hh.shape[1]), x.dtype)
            c0 = jnp.zeros_like(h0)

            def step(carry, xp):
                h, c = carry
                gates = xp + h @ W_hh.T
                i, f, g, o = jnp.split(gates, 4, axis=-1)
                c = jax.nn.sigmoid(f) * c + jax.nn.sigmoid(i) * jnp.tanh(g)
                h = jax.nn.sigmoid(o) * jnp.tanh(c)
                return ((h, c), h)
            _, hs = jax.lax.scan(step, (h0, c0), jnp.swapaxes(x_proj, 0, 1))
            return jnp.swapaxes(hs, 0, 1)
        lstm_out = _lstm(x, W_ih, W_hh, b_ih, b_hh)
        logits = jnp.einsum('bth,lh->btl', lstm_out, W_lin) + b_lin
        g = jax.lax.stop_gradient(jnp.argmax(logits, axis=-1).astype(lstm_out.dtype))[..., None]
        w = g * lstm_out
        inc = jnp.cumsum(w, axis=1)
        prefix = inc - w
        suffix = inc[:, -1:, :] - inc
        return 2.0 * lstm_out + prefix * fw_att + suffix * bw_att
    edge_index = jnp.stack([src, dst])
    x = x + _L0_gnn_ref(_layernorm(x, axis=-1), edge_weight, src, dst)
    x = x + _L0_ffn_ref(_layernorm(x, axis=-1)[None], L0_ffn_Wr, L0_ffn_br, L0_ffn_W1, L0_ffn_b1, L0_ffn_W2, L0_ffn_b2, L0_ffn_gamma, L0_ffn_beta)[0]
    x = x + _L1_gnn_ref(_layernorm(x, axis=-1), edge_index, L1_gnn_W, L1_gnn_b, L1_gnn_a_src, L1_gnn_a_dst)
    x = x + _L1_ffn_ref(_layernorm(x, axis=-1)[None], L1_ffn_W_ih, L1_ffn_W_hh, L1_ffn_b_ih, L1_ffn_b_hh, L1_ffn_W_lin, L1_ffn_b_lin, L1_ffn_fw_att, L1_ffn_bw_att)[0]
    return x

_drawn_inputs = setup_inputs


def setup_inputs(seed=0):
    import zlib

    import numpy as np

    out = dict(_drawn_inputs(seed))
    spreads = {'L0_ffn_br': (0.0, 0.1),
     'L0_ffn_b1': (0.0, 0.42),
     'L0_ffn_b2': (0.0, 0.269),
     'L0_ffn_gamma': (1.0, 0.2),
     'L0_ffn_beta': (0.0, 0.1),
     'L1_gnn_b': (0.0, 0.1),
     'L1_ffn_fw_att': (0.0010000000474974513, 0.6),
     'L1_ffn_bw_att': (0.0010000000474974513, 0.6)}
    factors = {'L0_ffn_Wr': 64.0,
     'L1_ffn_b_ih': 3.063,
     'L1_ffn_b_hh': 2.837,
     'L1_ffn_W_lin': 5.968,
     'L1_gnn_a_src': 2.669,
     'L1_ffn_b_lin': 3.526}
    for name, (base, spread) in spreads.items():
        noise = np.random.default_rng([zlib.crc32(name.encode()), seed]).standard_normal(out[name].shape)
        drawn = base * np.exp(spread * noise) if base else spread * noise
        out[name] = jnp.asarray(drawn.astype(out[name].dtype))
    for name, factor in factors.items():
        out[name] = (out[name] * factor).astype(out[name].dtype)
    return out
```

```python
from contextlib import ExitStack

import concourse.bass as bass
from concourse import mybir

F32 = mybir.dt.float32
BF16 = mybir.dt.bfloat16
I32 = mybir.dt.int32
ALU = mybir.AluOpType
ACT = mybir.ActivationFunctionType
AX = mybir.AxisListType
ds = bass.ds

P = 128
N = 6250
D = 256
E = 200000
NB = -(-N // P)
NP = NB * P
TAIL = N - (NB - 1) * P
GB = 7
NG = NB // GB
GN = GB * P
HEADS = 4
HD = D // HEADS
EP = 125
EC = E // EP
U = 16
HU = U // 2
NI = -(-((E - NB) // P + NB) // U) * U
RF = 3
WAYS = 4
BIG = 3.0e38
EPS = 1e-5
NEXP, FF = 8, 512
FC = FF // P
CAP = float(-(-N * 5 // (4 * NEXP)))
LU = 25
KU = 5


def own_wait(eng, g):
    eng.sem_inc(g["waits_carried"][eng.engine.name], 1)


def layer_norm_group(dve, nc, g, rows, out, t, base, i):
    step, mv, root, rstd, tmp = t["step"], t["mv"], t["root"], t["rstd"], t["tmp"]
    n = [0]

    def done(ins):
        n[0] += 1
        ins.then_inc(step, 1)

    def reads_last():
        dve.wait_ge(step, base + n[0])

    for u in range(GB):
        done(nc.vector.bn_stats(t["stats"][:, u, :], rows(u)))
    reads_last()
    own_wait(dve, g)
    for u in range(GB):
        done(nc.vector.bn_aggr(mv[:, u, :], t["stats"][:, u, :]))
    reads_last()
    done(nc.vector.tensor_scalar(t["ve"][:, :], mv[:, :, 1], EPS, None, ALU.add))
    dve.wait_ge(t["rooted"], i + 1)
    done(nc.vector.reciprocal(rstd[:, :], root[:, :]))
    reads_last()
    done(nc.vector.tensor_tensor(tmp[:, :], t["ve"][:, :], rstd[:, :], ALU.mult))
    reads_last()
    done(nc.vector.tensor_tensor(tmp[:, :], tmp[:, :], rstd[:, :], ALU.mult))
    reads_last()
    done(nc.vector.tensor_scalar(tmp[:, :], tmp[:, :], -0.5, 1.5, ALU.mult, ALU.add))
    reads_last()
    done(nc.vector.tensor_tensor(rstd[:, :], rstd[:, :], tmp[:, :], ALU.mult))
    reads_last()
    for u in range(GB):
        done(nc.vector.tensor_scalar(out(u), rows(u), mv[:, u, 0:1], rstd[:, u:u + 1], ALU.subtract, ALU.mult))


LN_STEPS = 3 * GB + 6
LN_VE = 2 * GB + 1


def root_group(act, nc, t, base):
    act.wait_ge(t["step"], base + LN_VE)
    nc.scalar.sqrt(t["root"][:, :], t["ve"][:, :]).then_inc(t["rooted"], 1)


def norm_tiles(sb, sem, tag):
    small = {k: sb(f"{tag}_{k}", [P, GB]) for k in ("ve", "root", "rstd", "tmp")}
    return {"rooted": sem(tag + "_rooted"), "step": sem(tag + "_step"), "stats": sb(tag + "_stats", [P, GB, 6]),
            "mv": sb(tag + "_mv", [P, GB, 2])} | small


def transpose_group(pe, nc, src, ident, tps, done):
    for c in range(2):
        for u in range(GB):
            nc.tensor.transpose(tps[2 * c + u // 4][:, (u % 4) * P:(u % 4 + 1) * P],
                                src[:, u, c * P:(c + 1) * P], ident[:, :]).then_inc(done, 1)


def copy_transposed(act, nc, tps, xt, done, base, copied):
    for c in range(2):
        for h, (a, n) in enumerate(((0, 4), (4, GB - 4))):
            act.wait_ge(done, base + c * GB + a + n)
            nc.scalar.copy(xt[:, c, a * P:(a + n) * P], tps[2 * c + h][:, 0:n * P]).then_inc(copied, 1)


def stage_normalise(nc, sb, sem, g):
    t = norm_tiles(sb, sem, "ln0")
    yt = sb("ln0_out", [P, GB, D])
    x_loaded, pads, step, stored, made = sem("x_loaded"), g["started"], t["step"], sem("y_stored"), sem("consts_made")
    with nc.Block() as block:
        @block.sync
        def _(sp):
            sp.wait_ge(pads, 1)
            sp.dma_start(g["X"][:, 0:NB - 1, :], g["x"][0:(NB - 1) * P, :].rearrange("(b p) d -> p b d", p=P)).then_inc(x_loaded, 16)
            sp.dma_start(g["X"][0:TAIL, NB - 1, :], g["x"][(NB - 1) * P:N, :]).then_inc(x_loaded, 16)
            with sp.Fori(0, NG) as i:
                sp.wait_ge(step, i * LN_STEPS + LN_STEPS)
                sp.dma_start(g["y"][ds(i * GN, GN), :].rearrange("(u p) d -> p u d", p=P), yt[:, :, :]).then_inc(stored, 16)
            sp.wait_ge(stored, 16 * NG + 16)

        @block.gpsimd
        def _(pool):
            pool.memset(g["ident"][:, :], 0.0).then_inc(made, 1)
            pool.iota(g["iota"][:, :], [[1, P]], base=0, channel_multiplier=0, allow_small_or_imprecise_dtypes=True).then_inc(made, 1)
            pool.memset(yt[:, 0, 0:1], 0.0).then_inc(stored, 16)
            pool.wait_ge(made, 2)
            pool.affine_select(out=g["ident"][:, :], in_=g["ident"][:, :], compare_op=ALU.not_equal, fill=1.0,
                               base=0, pattern=[[-1, P]], channel_multiplier=1).then_inc(made, 1)
            pool.wait_ge(made, 3)

        @block.scalar
        def _(act):
            with act.Fori(0, NG) as i:
                root_group(act, nc, t, i * LN_STEPS)

        @block.vector
        def _(dve):
            nc.vector.memset(g["X"][:, NB - 1:NB + 1, :], 0.0).then_inc(pads, 1)
            dve.wait_ge(pads, 1)
            dve.wait_ge(x_loaded, 32)
            with dve.Fori(0, NG) as i:
                dve.wait_ge(stored, i * 16 + 16)
                own_wait(dve, g)
                layer_norm_group(dve, nc, g, lambda u: g["X"][:, ds(i * GB + u, 1), :], lambda u: yt[:, u, :], t, i * LN_STEPS, i)


def stage_places(nc, sb, sem, g):
    src = sb("src_i", [EP, EC], I32)
    hi_i = sb("hi_i", [EP, EC], I32)
    hi = sb("hi", [EP, EC])
    dst = sb("dst_i", [EP, EC], I32)
    ew = sb("ew_in", [EP, EC])
    in_b = sb("in_b", [EP, EC], I32)
    rank = sb("rank", [EP, EC])
    pos = sb("pos", [EP, EC])
    pos_i = sb("pos_i", [EP, EC], I32)
    col_i = sb("col_i", [EP, EC], I32)
    zero = sb("zero", [P, NI * RF])
    upper = sb("upper", [P, P])
    ones = sb("ones_c", [P, P])
    cnt = sb("cnt", [EP, NB])
    tot = sb("tot", [P, NB])
    tot_i = sb("tot_i", [P, NB], I32)
    nit = sb("nit", [P, NB])
    cum = sb("cum", [P, NB])
    first = sb("first", [EP, NB])
    off = sb("off", [EP, NB])
    item = sb("item", [P, NI])
    counts_ps = g["ps"][0]
    loaded, ready, step, counted, summed, s_item, s_bw, s_bw2 = (sem(n) for n in (
        "edges_loaded", "sort_consts", "sort_step", "bucket_counted", "bucket_summed", "item_step", "s_bw", "s_bw2"))
    with nc.Block() as block:
        @block.sync
        def _(sp):
            sp.dma_start(src[:, :], g["src"].rearrange("(p c) -> p c", p=EP)).then_inc(loaded, 16)
            sp.dma_start(dst[:, :], g["dst"].rearrange("(p c) -> p c", p=EP)).then_inc(loaded, 16)
            sp.dma_start(ew[:, :], g["edge_weight"].rearrange("(p c) -> p c", p=EP)).then_inc(loaded, 16)

        @block.gpsimd
        def _(pool):
            pool.memset(zero[:, :], 0.0).then_inc(ready, 1)
            pool.memset(ones[:, :], 1.0).then_inc(ready, 1)
            pool.memset(upper[:, :], 1.0).then_inc(ready, 1)
            pool.iota(item[:, :], [[1, NI]], base=0, channel_multiplier=0, allow_small_or_imprecise_dtypes=True).then_inc(ready, 1)
            pool.wait_ge(ready, 4)
            for k in range(WAYS):
                pool.dma_start(g["rec"][k].rearrange("(p r) f -> p (r f)", p=P), zero[:, :]).then_inc(g["scattered"][k], 16)
            pool.affine_select(out=upper[:, :], in_=upper[:, :], compare_op=ALU.is_gt, fill=0.0, base=0,
                               pattern=[[1, P]], channel_multiplier=-1).then_inc(ready, 1)
            for k in range(WAYS):
                pool.wait_ge(g["scattered"][k], 16)

        @block.tensor
        def _(pe):
            pe.wait_ge(ready, 5)
            pe.wait_ge(counted, NB)
            nc.tensor.matmul(counts_ps[0:EP, 0:NB], upper[0:EP, 0:EP], cnt[:, :], start=True, stop=True)
            nc.tensor.matmul(g["ps"][1][:, 0:NB], ones[0:EP, :], cnt[:, :], start=True, stop=True).then_inc(summed, 1)

        @block.vector
        def _(dve):
            n = [0]

            def link(ins):
                n[0] += 1
                ins.then_inc(step, 1)
                dve.wait_ge(step, n[0])

            dve.wait_ge(loaded, 48)
            link(nc.vector.tensor_single_scalar(hi_i[:, :], src[:, :], 7, ALU.arith_shift_right))
            link(nc.vector.tensor_copy(hi[:, :], hi_i[:, :]))
            link(nc.vector.tensor_scalar(g["REC"][:, :, 0], src[:, :], 1.0, None, ALU.add))
            link(nc.vector.tensor_copy(g["REC"][:, :, 1], dst[:, :]))
            link(nc.vector.tensor_copy(g["REC"][:, :, 2], ew[:, :]))
            dve.wait_ge(ready, 5)
            with dve.Fori(0, NB) as b:
                nc.vector.tensor_scalar(rank[:, :], hi[:, :], item[0:EP, ds(b, 1)], 0.0, ALU.is_equal, ALU.add,
                                        accum_out=cnt[:, ds(b, 1)]).then_inc(counted, 1)
                dve.wait_ge(counted, b + 1)
            dve.wait_ge(summed, 1)
            link(nc.vector.tensor_copy(tot[:, :], g["ps"][1][:, 0:NB]))
            link(nc.vector.tensor_scalar(tot_i[:, :], tot[:, :], float(P - 1), None, ALU.add))
            link(nc.vector.tensor_single_scalar(tot_i[:, :], tot_i[:, :], 7, ALU.arith_shift_right))
            link(nc.vector.tensor_copy(nit[:, :], tot_i[:, :]))
            link(nc.vector.tensor_tensor_scan(cum[:, :], nit[:, :], nit[:, :], 0.0, ALU.add, ALU.bypass))
            link(nc.vector.tensor_tensor(first[:, :], cum[0:EP, :], nit[0:EP, :], ALU.subtract))
            link(nc.vector.tensor_scalar(first[:, :], first[:, :], float(P), -1.0, ALU.mult, ALU.add))
            link(nc.vector.tensor_tensor(off[:, :], first[:, :], counts_ps[0:EP, 0:NB], ALU.add))
            link(nc.vector.memset(g["BW"][:, :], 0.0))
            m0 = n[0]
            with dve.Fori(0, NB) as b:
                nc.vector.tensor_single_scalar(in_b[:, :], hi[:, :], item[0:EP, ds(b, 1)], ALU.is_equal).then_inc(s_item, 1)
                dve.wait_ge(s_item, b * 3 + 1)
                nc.vector.tensor_tensor_scan(rank[:, :], in_b[:, :], in_b[:, :], off[:, ds(b, 1)], ALU.add, ALU.bypass).then_inc(s_item, 1)
                nc.vector.scalar_tensor_tensor(out=g["BW"][:, :], in0=item[:, :], scalar=cum[:, ds(b, 1)], in1=g["BW"][:, :],
                                               op0=ALU.is_ge, op1=ALU.add).then_inc(s_bw, 1)
                dve.wait_ge(s_item, b * 3 + 2)
                own_wait(dve, g)
                nc.vector.copy_predicated(pos[:, :], in_b[:, :], rank[:, :]).then_inc(s_item, 1)
                dve.wait_ge(s_item, b * 3 + 3)
                dve.wait_ge(s_bw, b + 1)
            link(nc.vector.tensor_copy(pos_i[:, :], pos[:, :]))
            link(nc.vector.tensor_single_scalar(col_i[:, :], pos_i[:, :], 7, ALU.arith_shift_right))
            link(nc.vector.tensor_single_scalar(pos_i[:, :], pos_i[:, :], P - 1, ALU.bitwise_and))
            link(nc.vector.scalar_tensor_tensor(out=g["POS"][:, :], in0=pos_i[:, :], scalar=float(NI), in1=col_i[:, :],
                                                op0=ALU.mult, op1=ALU.add))


def stage_scatter(nc, sb, sem, g):
    recs = sb("st_rec", [EP, 2, HU, RF])
    idx = sb("st_idx", [EP, 2, HU], I32)
    staged = sem("scatter_staged")
    per = U // WAYS
    with nc.Block() as block:
        @block.scalar
        def _(act):
            with act.Fori(0, EC // U) as i:
                for h in range(2):
                    for k in range(WAYS):
                        act.wait_ge(g["scattered"][k], i * (16 * per) + 16 * (1 + h * per // 2))
                    nc.scalar.copy(recs[:, h, :, :], g["REC"][:, ds(i * U + h * HU, HU), :]).then_inc(staged, 1)
                    nc.scalar.copy(idx[:, h, :], g["POS"][:, ds(i * U + h * HU, HU)]).then_inc(staged, 1)

        @block.gpsimd
        def _(pool):
            with pool.Fori(0, EC // U) as i:
                for h in range(2):
                    for u in range(HU):
                        if u == 0:
                            pool.wait_ge(staged, i * 4 + (2 * h + 2))
                        k, turn = u % WAYS, (h * HU + u) // WAYS
                        pool.wait_ge(g["scattered"][k], i * (16 * per) + 16 * (1 + turn))
                        own_wait(pool, g)
                        pool.indirect_dma_start(g["rec"][k], bass.IndirectOffsetOnAxis(ap=idx[:, h, u:u + 1], axis=0),
                                                recs[:, h, u, :], None).then_inc(g["scattered"][k], 16)
            for k in range(WAYS):
                pool.wait_ge(g["scattered"][k], 16 * (1 + EC // WAYS))


def stage_items(nc, sb, sem, g):
    part = [sb(f"rec_part{k}", [P, NI * RF]) for k in range(WAYS)]
    loaded, step = sem("rec_loaded"), sem("items_step")
    with nc.Block() as block:
        @block.sync
        def _(sp):
            for k in range(WAYS):
                sp.dma_start(part[k][:, :], g["rec"][k].rearrange("(p r) f -> p (r f)", p=P)).then_inc(loaded, 16)

        @block.vector
        def _(dve):
            n = [0]

            def link(ins):
                n[0] += 1
                ins.then_inc(step, 1)
                dve.wait_ge(step, n[0])

            dve.wait_ge(loaded, 16 * WAYS)
            for k in range(1, WAYS):
                link(nc.vector.tensor_tensor(part[0][:, :], part[0][:, :], part[k][:, :], ALU.add))
            rec = part[0][:, :].rearrange("p (r f) -> p r f", f=RF)
            link(nc.vector.tensor_copy(g["DST"][:, 0:NI], rec[:, :, 1]))
            link(nc.vector.tensor_copy(g["EW"][:, 0:NI], rec[:, :, 2]))
            link(nc.vector.tensor_scalar(part[1][:, 0:NI], g["BW"][:, :], float(P), 1.0, ALU.mult, ALU.add))
            link(nc.vector.tensor_tensor(g["LO"][:, 0:NI], rec[:, :, 0], part[1][:, 0:NI], ALU.subtract))
            link(nc.vector.tensor_copy(g["BI"][0:1, 0:NI], g["BW"][0:1, :]))
            link(nc.vector.memset(g["BI"][0:1, NI:NI + U], NB))
            link(nc.vector.memset(g["DST"][:, NI:NI + U], 0))
            link(nc.vector.memset(g["LO"][:, NI:NI + U], -1.0))
            link(nc.vector.memset(g["EW"][:, NI:NI + U], 0.0))


def gather_rows(pool, nc, g, table, rows, idx, staged, freed, base):
    with pool.Fori(0, NI // U) as i:
        for u in range(U):
            if u % HU == 0:
                pool.wait_ge(staged, i * 2 + (u // HU + 1))
            pool.wait_ge(freed, i * U + (u + 1))
            own_wait(pool, g)
            pool.indirect_dma_start(rows[:, u, :], None, table,
                                    bass.IndirectOffsetOnAxis(ap=idx[:, u // HU, u % HU:u % HU + 1], axis=0)).then_inc(g["got"][u], 16)


def stage_indices(act, nc, g, idx, i, h, staged, freed):
    act.wait_ge(freed, i * U + (h + 1) * HU)
    nc.scalar.copy(idx[:, h, :], g["DST"][:, ds(i * U + h * HU, HU)]).then_inc(staged, 1)


def stage_aggregate(nc, sb, sem, g):
    idx = sb("ag_idx", [P, 2, HU], I32)
    rows = sb("ag_rows", [P, U, D])
    pick = sb("ag_pick", [P, U, P])
    free = sb("ag_free", [1, 2])
    sums = [g["ps"][k][:, 0:D] for k in range(4)]
    staged, picked, summed, added = (sem(n) for n in ("ag_staged", "ag_picked", "ag_summed", "ag_added"))
    with nc.Block() as block:
        @block.scalar
        def _(act):
            with act.Fori(0, NI // U) as i:
                for h in range(2):
                    stage_indices(act, nc, g, idx, i, h, staged, summed)

        @block.gpsimd
        def _(pool):
            pool.memset(free[:, 0:1], 0.0).then_inc(summed, U)
            gather_rows(pool, nc, g, g["y"], rows, idx, staged, summed, 0)

        @block.tensor
        def _(pe):
            with pe.Fori(0, NI // U) as i:
                for u in range(U):
                    pe.wait_ge(picked, i * U + (u + 1))
                    pe.wait_ge(added, i * U + (u + 1))
                    pe.wait_ge(g["got"][u], i * 16 + 16)
                    nc.tensor.matmul(sums[u % 4], pick[:, u, :], rows[:, u, :], start=True, stop=True).then_inc(summed, 1)

        @block.vector
        def _(dve):
            def picks(i, h):
                for u in range(h * HU, (h + 1) * HU):
                    dve.wait_ge(summed, i * U + (u + 1))
                    w = i * U + u
                    nc.vector.tensor_scalar(pick[:, u, :], g["iota"][:, :], g["LO"][:, ds(w, 1)], g["EW"][:, ds(w, 1)],
                                            ALU.is_equal, ALU.mult).then_inc(picked, 1)

            def adds(i, h):
                for u in range(h * HU, (h + 1) * HU):
                    b = nc.vector.value_load(g["BI"][0:1, ds(i * U + u, 1)], min_val=0, max_val=NB)
                    dve.wait_ge(summed, i * U + (U + u + 1))
                    dve.wait_ge(added, i * U + (u + 4))
                    nc.vector.tensor_tensor(g["X"][:, ds(b, 1), :], g["X"][:, ds(b, 1), :], sums[u % 4], ALU.add).then_inc(added, 1)

            nc.vector.memset(free[:, 1:2], 0.0).then_inc(added, 4)
            picks(0, 0)
            with dve.Fori(0, NI // U) as i:
                picks(i, 1)
                adds(i, 0)
                picks(i + 1, 0)
                adds(i, 1)


def stage_experts(nc, sb, sem, g):
    t = norm_tiles(sb, sem, "ln1")
    t2 = norm_tiles(sb, sem, "ln2")
    xn = sb("moe_xn", [P, NB, D])
    xt = sb("moe_xt", [P, 2, GN])
    hid = sb("moe_hid", [P, 2 * FC, GN])
    w1 = sb("moe_w1", [P, 2, 2, FF])
    w2 = sb("moe_w2", [P, 2, FC, D])
    b1 = sb("moe_b1", [P, 2, FC])
    b2 = sb("moe_b2", [P, 2, D])
    gam, bet = sb("moe_gamma", [P, D]), sb("moe_beta", [P, D])
    wr = sb("moe_wr", [P, 2, NEXP])
    row = {k: sb("moe_" + k, [1, NEXP]) for k in ("br", "lg", "ex", "rw", "sc", "el", "eq", "io", "cd", "rw2")}
    sc1 = {k: sb("moe1_" + k, [1, 1]) for k in ("mx", "sm", "rc")}
    top, idx_f, idx_i = sb("moe_top", [1, 2]), sb("moe_idxf", [1, 2]), sb("moe_idxi", [1, 2], I32)
    wts, wb = sb("moe_wts", [1, 2]), sb("moe_wb", [P, 2])
    mrow, mcol, ones, onef = sb("moe_mrow", [1, D]), sb("moe_mcol", [P, 2]), sb("moe_ones", [P, 1]), sb("moe_onesr", [1, P])
    v, nv = sb("moe_v", [P, GB, D]), sb("moe_nv", [P, GB, D])
    small, big, made, meant, mean_c, meanT, mcopied, logit, exp_in, exp_out = (sem("moe_" + n) for n in (
        "small", "big", "made", "meant", "mean_c", "meanT", "mcopied", "logit", "exp_in", "exp_out"))
    route, weighted, spread, trans, copied, h_ready, gelud, o_ready, evac, fin = (sem("moe_" + n) for n in (
        "route", "weighted", "spread", "trans", "copied", "h_ready", "gelud", "o_ready", "evac", "fin"))
    picked, scaled, v_ready = sem("moe_picked"), sem("moe_scaled"), sem("moe_v_ready")
    step = sem("moe_step")
    ps = g["ps"]
    half = GN // 2
    with nc.Block() as block:
        @block.sync
        def _(sp):
            sp.dma_start(wr[:, :, :], g["L0_ffn_Wr"].rearrange("(c p) e -> p c e", p=P)).then_inc(small, 16)
            sp.dma_start(row["br"][:, :], g["L0_ffn_br"].rearrange("(a e) -> a e", a=1)).then_inc(small, 16)
            sp.dma_start(gam[:, :], g["L0_ffn_gamma"].rearrange("(a e) -> a e", a=1).to_broadcast([P, D])).then_inc(small, 16)
            sp.dma_start(bet[:, :], g["L0_ffn_beta"].rearrange("(a e) -> a e", a=1).to_broadcast([P, D])).then_inc(small, 16)
            sp.wait_ge(picked, 1)
            for k in range(2):
                e = nc.sync.value_load(idx_i[0:1, k:k + 1], min_val=0, max_val=NEXP - 1)
                sp.dma_start(w1[:, k, :, :], g["L0_ffn_W1"][ds(e, 1), :, :].rearrange("a (c p) f -> p (a c) f", p=P)).then_inc(big, 16)
                sp.dma_start(w2[:, k, :, :], g["L0_ffn_W2"][ds(e, 1), :, :].rearrange("a (c p) d -> p (a c) d", p=P)).then_inc(big, 16)
                sp.dma_start(b1[:, k, :], g["L0_ffn_b1T"][:, ds(e, 1), :].rearrange("p a c -> p (a c)")).then_inc(big, 16)
                sp.dma_start(b2[:, k, :], g["L0_ffn_b2"][ds(e, 1), :].to_broadcast([P, D])).then_inc(big, 16)

        @block.gpsimd
        def _(pool):
            pool.memset(ones[:, :], 1.0).then_inc(made, 1)
            pool.memset(onef[:, :], 1.0).then_inc(made, 1)
            pool.iota(row["io"][:, :], [[1, NEXP]], base=0, channel_multiplier=0, allow_small_or_imprecise_dtypes=True).then_inc(made, 1)
            pool.memset(v[:, :, :], 0.0).then_inc(trans, 2 * GB)
            pool.wait_ge(t["step"], NG * LN_STEPS)
            with pool.Fori(0, NG) as i:
                pool.wait_ge(trans, i * (2 * GB) + 2 * GB)
                nc.gpsimd.tensor_copy(v[:, :, :], xn[:, ds(i * GB, GB), :]).then_inc(v_ready, 1)

        @block.tensor
        def _(pe):
            pe.wait_ge(made, 3)
            pe.wait_ge(t["step"], NG * LN_STEPS)
            nc.tensor.matmul(ps[0][0:1, 0:D], ones[:, 0:1], xn[:, 0, :], start=True, stop=False)
            with pe.Fori(1, NB - 1) as b:
                nc.tensor.matmul(ps[0][0:1, 0:D], ones[:, 0:1], xn[:, ds(b, 1), :], start=False, stop=False)
            nc.tensor.matmul(ps[0][0:1, 0:D], ones[0:TAIL, 0:1], xn[0:TAIL, NB - 1, :], start=False, stop=True).then_inc(meant, 1)
            pe.wait_ge(mean_c, 1)
            for c in range(2):
                nc.tensor.matmul(ps[1][:, c:c + 1], mrow[0:1, c * P:(c + 1) * P], onef[0:1, 0:1], start=True, stop=True).then_inc(meanT, 1)
            pe.wait_ge(mcopied, 1)
            pe.wait_ge(small, 64)
            for c in range(2):
                nc.tensor.matmul(ps[2][0:1, 0:NEXP], mcol[:, c:c + 1], wr[:, c, :], start=c == 0, stop=c == 1).then_inc(logit, 1)
            pe.wait_ge(weighted, 1)
            nc.tensor.matmul(ps[3][:, 0:2], onef[0:1, :], wts[0:1, :], start=True, stop=True).then_inc(spread, 1)
            pe.wait_ge(scaled, 1)
            with pe.Fori(0, NG) as i:
                pe.wait_ge(v_ready, i + 1)
                transpose_group(pe, nc, v, g["ident"], ps, trans)
                pe.wait_ge(copied, i * 4 + 4)
                for q in range(4 * FC):
                    k, s, f = q // (2 * FC), q // FC % 2, q % FC
                    pe.wait_ge(gelud, i * (4 * FC) + (q + 1))
                    for c in range(2):
                        m = nc.tensor.matmul(ps[4 + q % 2][:, 0:half], w1[:, k, c, f * P:(f + 1) * P], xt[:, c, s * half:(s + 1) * half],
                                             start=c == 0, stop=c == 1)
                    m.then_inc(h_ready, 1)
                pe.wait_ge(gelud, i * (4 * FC) + (4 * FC + 2))
                for u in range(GB):
                    pe.wait_ge(evac, i * GB + (u + 1))
                    for q in range(2 * FC):
                        m = nc.tensor.matmul(ps[6 + u % 2][:, 0:D], hid[:, q, u * P:(u + 1) * P], w2[:, q // FC, q % FC, :],
                                             start=q == 0, stop=q == 2 * FC - 1)
                    m.then_inc(o_ready, 1)

        @block.scalar
        def _(act):
            with act.Fori(0, NG) as i:
                root_group(act, nc, t, i * LN_STEPS)
            act.wait_ge(meant, 1)
            nc.scalar.mul(mrow[:, :], ps[0][0:1, 0:D], 1.0 / N).then_inc(mean_c, 1)
            act.wait_ge(meanT, 2)
            nc.scalar.copy(mcol[:, :], ps[1][:, 0:2]).then_inc(mcopied, 1)
            for n in range(2):
                act.wait_ge(exp_in, n + 1)
                nc.scalar.activation(row["ex"][:, :], row["sc"][:, :], ACT.Exp).then_inc(exp_out, 1)
            act.wait_ge(exp_in, 3)
            nc.scalar.activation(wts[:, :], top[:, :], ACT.Exp).then_inc(exp_out, 1)
            act.wait_ge(big, 16 * 8)
            with act.Fori(0, NG) as i:
                copy_transposed(act, nc, ps, xt, trans, i * (2 * GB) + 2 * GB, copied)
                for q in range(4 * FC):
                    k, s, f = q // (2 * FC), q // FC % 2, q % FC
                    act.wait_ge(h_ready, i * (4 * FC) + (q + 1))
                    nc.scalar.activation(hid[:, k * FC + f, s * half:(s + 1) * half], ps[4 + q % 2][:, 0:half], ACT.Gelu,
                                         bias=b1[:, k, f:f + 1]).then_inc(gelud, 1)
                root_group(act, nc, t2, i * LN_STEPS)

        @block.vector
        def _(dve):
            n = [0]

            def link(ins):
                n[0] += 1
                ins.then_inc(step, 1)
                dve.wait_ge(step, n[0])

            with dve.Fori(0, NG) as i:
                layer_norm_group(dve, nc, g, lambda u: g["X"][:, ds(i * GB + u, 1), :], lambda u: xn[:, ds(i * GB + u, 1), :], t, i * LN_STEPS, i)
            vec = nc.vector
            r = row
            dve.wait_ge(logit, 2)
            dve.wait_ge(small, 64)
            dve.wait_ge(made, 3)
            link(vec.tensor_tensor(r["lg"][:, :], ps[2][0:1, 0:NEXP], r["br"][:, :], ALU.add))

            def softmax(src, dst, turn):
                link(vec.tensor_reduce(sc1["mx"][:, :], src[:, :], AX.X, ALU.max))
                vec.tensor_scalar(r["sc"][:, :], src[:, :], sc1["mx"][:, 0:1], None, ALU.subtract).then_inc(exp_in, 1)
                dve.wait_ge(exp_out, turn)
                link(vec.tensor_reduce(sc1["sm"][:, :], r["ex"][:, :], AX.X, ALU.add))
                link(vec.reciprocal(sc1["rc"][:, :], sc1["sm"][:, :]))
                link(vec.tensor_scalar(dst[:, :], r["ex"][:, :], sc1["rc"][:, 0:1], None, ALU.mult))

            softmax(r["lg"], r["rw"], 1)
            link(vec.tensor_scalar(r["el"][:, :], r["rw"][:, :], float(N), None, ALU.mult))
            link(vec.tensor_scalar(r["cd"][:, :], r["el"][:, :], CAP, None, ALU.max))
            link(vec.reciprocal(r["eq"][:, :], r["cd"][:, :]))
            link(vec.tensor_scalar(r["eq"][:, :], r["eq"][:, :], CAP, -1.0, ALU.mult, ALU.add))
            link(vec.tensor_scalar(r["cd"][:, :], r["el"][:, :], CAP, None, ALU.is_gt))
            link(vec.tensor_tensor(r["eq"][:, :], r["eq"][:, :], r["cd"][:, :], ALU.mult))
            link(vec.tensor_scalar(r["eq"][:, :], r["eq"][:, :], 1.0, None, ALU.add))
            link(vec.tensor_tensor(r["rw"][:, :], r["rw"][:, :], r["eq"][:, :], ALU.mult))
            softmax(r["rw"], r["rw2"], 2)
            for k in range(2):
                link(vec.tensor_reduce(top[:, k:k + 1], r["rw2"][:, :], AX.X, ALU.max))
                link(vec.tensor_scalar(r["eq"][:, :], r["rw2"][:, :], top[:, k:k + 1], float(NEXP), ALU.is_lt, ALU.mult))
                link(vec.tensor_tensor(r["cd"][:, :], r["eq"][:, :], r["io"][:, :], ALU.add))
                link(vec.tensor_reduce(idx_f[:, k:k + 1], r["cd"][:, :], AX.X, ALU.min))
                link(vec.tensor_scalar(r["eq"][:, :], r["io"][:, :], idx_f[:, k:k + 1], -4.0, ALU.is_equal, ALU.mult))
                link(vec.tensor_tensor(r["rw2"][:, :], r["rw2"][:, :], r["eq"][:, :], ALU.add))
            vec.tensor_copy(idx_i[:, :], idx_f[:, :]).then_inc(picked, 1)
            link(vec.tensor_scalar(sc1["mx"][:, :], top[:, 0:1], 1.0, None, ALU.mult))
            vec.tensor_scalar(top[:, :], top[:, :], sc1["mx"][:, 0:1], None, ALU.subtract).then_inc(exp_in, 1)
            dve.wait_ge(exp_out, 3)
            link(vec.tensor_reduce(sc1["sm"][:, :], wts[:, :], AX.X, ALU.add))
            link(vec.reciprocal(sc1["rc"][:, :], sc1["sm"][:, :]))
            vec.tensor_scalar(wts[:, :], wts[:, :], sc1["rc"][:, 0:1], None, ALU.mult).then_inc(weighted, 1)
            dve.wait_ge(spread, 1)
            link(vec.tensor_copy(wb[:, :], ps[3][:, 0:2]))
            dve.wait_ge(big, 16 * 8)
            for k in range(2):
                link(vec.tensor_scalar(w2[:, k, :, :], w2[:, k, :, :], wb[:, k:k + 1], None, ALU.mult))
                link(vec.tensor_scalar(b2[:, k, :], b2[:, k, :], wb[:, k:k + 1], None, ALU.mult))
            link(vec.tensor_tensor(b2[:, 0, :], b2[:, 0, :], b2[:, 1, :], ALU.add))
            vec.memset(sc1["mx"][:, :], 0.0).then_inc(gelud, 2)
            vec.memset(sc1["sm"][:, :], 0.0).then_inc(evac, 2)
            vec.memset(sc1["rc"][:, :], 0.0).then_inc(scaled, 1)
            per = 4 * GB
            with dve.Fori(0, NG) as i:
                m = [0]

                def done(ins):
                    m[0] += 1
                    ins.then_inc(fin, 1)

                for u in range(GB):
                    dve.wait_ge(o_ready, i * GB + (u + 1))
                    vec.tensor_tensor(nv[:, u, :], ps[6 + u % 2][:, 0:D], b2[:, 0, :], ALU.add).then_inc(evac, 1)
                for u in range(GB):
                    dve.wait_ge(evac, i * GB + (u + 3))
                    done(vec.tensor_tensor(nv[:, u, :], nv[:, u, :], xn[:, ds(i * GB + u, 1), :], ALU.add))
                dve.wait_ge(fin, i * per + GB)
                own_wait(dve, g)
                layer_norm_group(dve, nc, g, lambda u: nv[:, u, :], lambda u: nv[:, u, :], t2, i * LN_STEPS, i)
                dve.wait_ge(t2["step"], i * LN_STEPS + LN_STEPS)
                for u in range(GB):
                    done(vec.tensor_tensor(nv[:, u, :], nv[:, u, :], gam[:, :], ALU.mult))
                dve.wait_ge(fin, i * per + 2 * GB)
                for u in range(GB):
                    done(vec.tensor_tensor(nv[:, u, :], nv[:, u, :], bet[:, :], ALU.add))
                dve.wait_ge(fin, i * per + 3 * GB)
                for u in range(GB):
                    done(vec.tensor_tensor(g["X"][:, ds(i * GB + u, 1), :], g["X"][:, ds(i * GB + u, 1), :], nv[:, u, :], ALU.add))
                dve.wait_ge(fin, i * per + per)

def stage_heads(nc, sb, sem, g):
    t = norm_tiles(sb, sem, "ln3")
    xn, xt = sb("wh_xn", [P, GB, D]), sb("wh_xt", [P, 2, GN])
    w = sb("wh_w", [P, 2, D])
    bias, a_src, a_dst = (sb("wh_" + k, [P, D]) for k in ("bias", "asrc", "adst"))
    wh, prod = sb("wh_out", [P, GB, D]), sb("wh_prod", [P, 2, D])
    ad = sb("wh_ad", [P, NB, HEADS])
    loaded, trans, copied, whole, step, stored, ad_stored, evac = (sem("wh_" + n) for n in (
        "loaded", "trans", "copied", "whole", "step", "stored", "ad_stored", "evac"))
    ps = g["ps"]
    with nc.Block() as block:
        @block.sync
        def _(sp):
            sp.dma_start(w[:, :, :], g["L1_gnn_W_T"].rearrange("(c p) d -> p c d", p=P)).then_inc(loaded, 16)
            for tile, name in ((bias, "L1_gnn_b"), (a_src, "L1_gnn_a_src"), (a_dst, "L1_gnn_a_dst")):
                sp.dma_start(tile[:, :], g[name].to_broadcast([P, D])).then_inc(loaded, 16)
            with sp.Fori(0, NG) as i:
                sp.wait_ge(evac, i * GB + 2 * GB)
                sp.dma_start(g["wh"][ds(i * GN, GN), :].rearrange("(u p) d -> p u d", p=P), wh[:, :, :]).then_inc(stored, 16)
            sp.wait_ge(step, NB * 4)
            sp.dma_start(g["ad"].rearrange("(b p) h -> p b h", p=P), ad[:, :, :]).then_inc(ad_stored, 16)
            sp.wait_ge(ad_stored, 16)
            sp.wait_ge(stored, 16 * NG)

        @block.tensor
        def _(pe):
            pe.wait_ge(loaded, 64)
            with pe.Fori(0, NG) as i:
                pe.wait_ge(t["step"], i * LN_STEPS + LN_STEPS)
                transpose_group(pe, nc, xn, g["ident"], ps, trans)
                pe.wait_ge(copied, i * 4 + 4)
                for u in range(GB):
                    pe.wait_ge(evac, i * GB + (GB + u - 3))
                    for c in range(2):
                        m = nc.tensor.matmul(ps[4 + u % 4][:, 0:D], xt[:, c, u * P:(u + 1) * P], w[:, c, :], start=c == 0, stop=c == 1)
                    m.then_inc(whole, 1)
                pe.wait_ge(evac, i * GB + 2 * GB)

        @block.scalar
        def _(act):
            with act.Fori(0, NG) as i:
                root_group(act, nc, t, i * LN_STEPS)
                copy_transposed(act, nc, ps, xt, trans, i * (2 * GB), copied)

        @block.vector
        def _(dve):
            vec = nc.vector
            vec.memset(g["AS"][:, NB:NB + 1, :], 0.0).then_inc(evac, GB)
            dve.wait_ge(evac, GB)
            dve.wait_ge(loaded, 64)
            with dve.Fori(0, NG) as i:
                layer_norm_group(dve, nc, g, lambda u: g["X"][:, ds(i * GB + u, 1), :], lambda u: xn[:, u, :], t, i * LN_STEPS, i)
                for u in range(GB):
                    dve.wait_ge(whole, i * GB + (u + 1))
                    vec.tensor_tensor(wh[:, u, :], ps[4 + u % 4][:, 0:D], bias[:, :], ALU.add).then_inc(evac, 1)
                for u in range(GB):
                    dve.wait_ge(evac, i * GB + (GB + u + 1))
                    for k, a in ((0, a_src), (1, a_dst)):
                        vec.tensor_tensor(prod[:, k, :], wh[:, u, :], a[:, :], ALU.mult).then_inc(step, 1)
                    for k in range(2):
                        dve.wait_ge(step, i * (4 * GB) + (4 * u + k + 1))
                        out = g["AS"][:, ds(i * GB + u, 1), 0:HEADS] if k == 0 else ad[:, ds(i * GB + u, 1), :]
                        vec.tensor_reduce(out.rearrange("p a h -> p (a h)"), prod[:, k, :].rearrange("p (h d) -> p h d", h=HEADS),
                                          AX.X, ALU.add).then_inc(step, 1)
                    dve.wait_ge(step, i * (4 * GB) + 4 * (u + 1))
                dve.wait_ge(stored, i * 16 + 16)


def stage_maxima(nc, sb, sem, g):
    idx = sb("mx_idx", [P, 2, HU], I32)
    adr = sb("mx_rows", [P, U, HEADS])
    R = 8
    pick = sb("mx_pick", [P, R, P])
    pen = sb("mx_pen", [P, R, P], BF16)
    diag = sb("mx_diag", [P, R, HEADS, P])
    ident4 = sb("mx_ident4", [P, HEADS, P], BF16)
    best = sb("mx_best", [P, R, HEADS])
    mx = sb("mx_table", [P, NB + 1, HEADS])
    free = sb("mx_free", [1, 1])
    staged, kept, picked, crossed, penned, diag_v, summed, reduced, stepped, consts = (sem("mx_" + n) for n in (
        "staged", "kept", "picked", "crossed", "penned", "diag_v", "summed", "reduced", "stepped", "consts"))
    ps = g["ps"]
    got0 = 16 * (NI // U)
    VH = 2
    with nc.Block() as block:
        @block.gpsimd
        def _(pool):
            pool.memset(free[:, :], 0.0).then_inc(summed, U)
            gather_rows(pool, nc, g, g["ad"], adr, idx, staged, summed, 0)

        @block.scalar
        def _(act):
            act.wait_ge(consts, 3)
            with act.Fori(0, NI // U) as i:
                for h in range(2):
                    stage_indices(act, nc, g, idx, i, h, staged, summed)
                for h in range(2):
                    for u in range(h * HU, (h + 1) * HU):
                        act.wait_ge(g["got"][u], i * 16 + (got0 + 16))
                    nc.scalar.copy(g["ADE"][:, ds(i * U + h * HU, HU), :], adr[:, h * HU:(h + 1) * HU, :]).then_inc(kept, 1)
                    for u in range(h * HU, (h + 1) * HU):
                        act.wait_ge(summed, i * U + (u + U - R + 1))
                        for k in range(VH, HEADS):
                            nc.scalar.activation(diag[:, u % R, k, :], g["ident"][:, :], ACT.Copy, scale=adr[:, u, k:k + 1]).then_inc(crossed, 1)
                        act.wait_ge(picked, i * U + (u + 1))
                        nc.scalar.activation(pen[:, u % R, :], pick[:, u % R, :], ACT.Copy, scale=BIG, bias=-BIG).then_inc(penned, 1)

        @block.tensor
        def _(pe):
            pe.wait_ge(consts, 3)
            with pe.Fori(0, NI // U) as i:
                for u in range(U):
                    pe.wait_ge(reduced, i * U + (u + 1))
                    pe.wait_ge(penned, i * U + (u + 1))
                    nc.tensor.matmul(ps[u % 8][:, :], pen[:, u % R, :], ident4[:, :, :].rearrange("p h e -> p (h e)"), start=True, stop=False)
                    pe.wait_ge(diag_v, i * U + (u + 1))
                    pe.wait_ge(crossed, i * (U * (HEADS - VH)) + (u + 1) * (HEADS - VH))
                    nc.tensor.matmul(ps[u % 8][:, :], pick[:, u % R, :], diag[:, u % R, :, :].rearrange("p h e -> p (h e)"),
                                     start=False, stop=True).then_inc(summed, 1)

        @block.vector
        def _(dve):
            vec = nc.vector
            vec.memset(mx[:, :, :], -BIG).then_inc(consts, 1)
            for k in range(HEADS):
                c = vec.tensor_copy(ident4[:, k, :], g["ident"][:, :])
            c.then_inc(consts, 1)
            vec.memset(best[:, :, :], 0.0).then_inc(reduced, 8)
            vec.memset(g["ADE"][:, NI:NI + U, :], 0.0).then_inc(consts, 1)
            dve.wait_ge(consts, 3)
            dve.wait_ge(reduced, 8)

            def prepare(i, u):
                dve.wait_ge(summed, i * U + (u + U - R + 1))
                vec.tensor_scalar(pick[:, u % R, :], g["iota"][:, :], g["LO"][:, ds(i * U + u, 1)], None, ALU.is_equal).then_inc(picked, 1)
                dve.wait_ge(g["got"][u], i * 16 + (got0 + 16))
                vec.tensor_tensor(diag[:, u % R, 0:VH, :], g["ident"][:, :].rearrange("p (a e) -> p a e", a=1).to_broadcast([P, VH, P]),
                                  adr[:, u, 0:VH].rearrange("p (h a) -> p h a", a=1).to_broadcast([P, VH, P]), ALU.mult).then_inc(diag_v, 1)

            def reduce(i, u):
                dve.wait_ge(summed, i * U + (U + u + 1))
                vec.tensor_reduce(best[:, u % R, :], ps[u % 8][:, :].rearrange("p (h e) -> p h e", h=HEADS), AX.X, ALU.max).then_inc(reduced, 1)

            def merge(i, u):
                b = vec.value_load(g["BI"][0:1, ds(i * U + u, 1)], min_val=0, max_val=NB)
                dve.wait_ge(reduced, i * U + (8 + u + 1))
                dve.wait_ge(stepped, i * U + (u + 1))
                vec.tensor_tensor(mx[:, ds(b, 1), :].rearrange("p a h -> p (a h)"), mx[:, ds(b, 1), :].rearrange("p a h -> p (a h)"), best[:, u % R, :], ALU.max).then_inc(stepped, 1)

            vec.memset(best[:, 0, 0:1], 0.0).then_inc(stepped, 1)
            LAG = 4
            with dve.Fori(0, NI // U) as i:
                for u in range(U + LAG + 1):
                    if u < U:
                        prepare(i, u)
                    if LAG <= u < U + LAG:
                        reduce(i, u - LAG)
                    if u > LAG:
                        merge(i, u - LAG - 1)
            dve.wait_ge(stepped, NI + 1)
            vec.tensor_tensor(mx[:, :, :], mx[:, :, :], g["AS"][:, :, 0:HEADS], ALU.add).then_inc(stepped, 1)
            dve.wait_ge(stepped, NI + 2)
            vec.scalar_tensor_tensor(out=g["AS"][:, :, HEADS:2 * HEADS], in0=mx[:, :, :], scalar=0.2, in1=mx[:, :, :],
                                     op0=ALU.mult, op1=ALU.max).then_inc(stepped, 1)


def stage_attend(nc, sb, sem, g):
    idx = sb("at_idx", [P, 2, HU], I32)
    rows = sb("at_rows", [P, U, D])
    pick = sb("at_pick", [P, U, P])
    pick_t = sb("at_pick_t", [P, HU, P])
    ex = sb("at_ex", [P, 2, HU, HEADS])
    z = sb("at_z", [P, 2, HU, HEADS])
    msg = sb("at_msg", [P, HU, D + HEADS])
    free = sb("at_free", [1, 3])
    staged, picked, turned, tcopied, ea_done, soft, exped, messaged, summed, added = (sem("at_" + n) for n in (
        "staged", "picked", "turned", "tcopied", "ea_done", "soft", "exped", "messaged", "summed", "added"))
    ps = g["ps"]
    tp = [ps[0], ps[1]]
    ea = [ps[2], ps[3]]
    sums = [ps[4 + k] for k in range(4)]
    got0 = 2 * 16 * (NI // U)
    W = D + HEADS

    def after(i, h):
        return (i, 1) if h == 0 else (i + 1, 0)

    with nc.Block() as block:
        @block.gpsimd
        def _(pool):
            pool.memset(free[:, 0:1], 0.0).then_inc(summed, U)
            gather_rows(pool, nc, g, g["wh"], rows, idx, staged, summed, 0)

        @block.scalar
        def _(act):
            def indices(i, h):
                nc.scalar.copy(idx[:, h, :], g["DST"][:, ds(i * U + h * HU, HU)]).then_inc(staged, 1)

            def turn_and_exp(i, h):
                for q in range(2):
                    act.wait_ge(turned, i * 4 + (2 * h + q + 1))
                    nc.scalar.copy(pick_t[:, 4 * q:4 * q + 4, :].rearrange("p u e -> p (u e)"), tp[q][:, :]).then_inc(tcopied, 1)
                act.wait_ge(soft, i * 8 + (4 * h + 4))
                nc.scalar.activation(ex[:, h, :, :], z[:, h, :, :], ACT.Exp).then_inc(exped, 1)

            indices(0, 0)
            turn_and_exp(0, 0)
            with act.Fori(0, NI // U) as i:
                for h in range(2):
                    act.wait_ge(summed, i * U + (U + h * HU))
                    indices(*after(i, h))
                    turn_and_exp(*after(i, h))

        @block.tensor
        def _(pe):
            def scores(i, h):
                for q in range(2):
                    for k in range(4):
                        u = h * HU + 4 * q + k
                        pe.wait_ge(picked, i * U + (u + 1))
                        m = nc.tensor.transpose(tp[q][:, k * P:(k + 1) * P], pick[:, u, :], g["ident"][:, :])
                    m.then_inc(turned, 1)
                for q in range(2):
                    pe.wait_ge(tcopied, i * 4 + (2 * h + q + 1))
                    for k in range(4):
                        u = 4 * q + k
                        b = nc.tensor.value_load(g["BI"][0:1, ds(i * U + h * HU + u, 1)], min_val=0, max_val=NB)
                        m = nc.tensor.matmul(ea[h][:, u * 2 * HEADS:(u + 1) * 2 * HEADS], pick_t[:, u, :],
                                             g["AS"][:, ds(b, 1), :].rearrange("p a h -> p (a h)"), start=True, stop=True)
                m.then_inc(ea_done, 1)

            scores(0, 0)
            with pe.Fori(0, NI // U) as i:
                for h in range(2):
                    scores(*after(i, h))
                    for k in range(HU):
                        u = h * HU + k
                        pe.wait_ge(messaged, i * U + (u + 1))
                        pe.wait_ge(added, i * U + (u + 1))
                        nc.tensor.matmul(sums[u % 4][:, 0:W], pick[:, u, :], msg[:, k, :], start=True, stop=True).then_inc(summed, 1)

        @block.vector
        def _(dve):
            vec = nc.vector

            def picks(i, h):
                for u in range(h * HU, (h + 1) * HU):
                    vec.tensor_scalar(pick[:, u, :], g["iota"][:, :], g["LO"][:, ds(i * U + u, 1)], None, ALU.is_equal).then_inc(picked, 1)

            def softmax(i, h):
                e = ea[h][:, 0:HU * 2 * HEADS].rearrange("p (u k) -> p u k", u=HU)
                zz = z[:, h, :, :]
                dve.wait_ge(ea_done, i * 2 + (h + 1))
                vec.tensor_tensor(zz, e[:, :, 0:HEADS], g["ADE"][:, ds(i * U + h * HU, HU), :], ALU.add).then_inc(soft, 1)
                dve.wait_ge(soft, i * 8 + (4 * h + 1))
                vec.scalar_tensor_tensor(out=zz, in0=zz, scalar=0.2, in1=zz, op0=ALU.mult, op1=ALU.max).then_inc(soft, 1)
                dve.wait_ge(soft, i * 8 + (4 * h + 2))
                vec.tensor_tensor(zz, zz, e[:, :, HEADS:2 * HEADS], ALU.subtract).then_inc(soft, 1)
                dve.wait_ge(soft, i * 8 + (4 * h + 3))
                vec.tensor_scalar(zz, zz, 0.0, None, ALU.min).then_inc(soft, 1)

            def messages(i, h):
                dve.wait_ge(exped, i * 2 + (h + 1))
                vec.tensor_copy(msg[:, :, D:W], ex[:, h, :, :])
                for k in range(HU):
                    u = h * HU + k
                    dve.wait_ge(g["got"][u], i * 16 + (got0 + 16))
                    vec.tensor_tensor(msg[:, k, 0:D].rearrange("p (h d) -> p h d", h=HEADS),
                                      rows[:, u, :].rearrange("p (h d) -> p h d", h=HEADS),
                                      ex[:, h, k, :].rearrange("p (h a) -> p h a", a=1).to_broadcast([P, HEADS, HD]), ALU.mult).then_inc(messaged, 1)

            def adds(i, h):
                for u in range(h * HU, (h + 1) * HU):
                    b = vec.value_load(g["BI"][0:1, ds(i * U + u, 1)], min_val=0, max_val=NB)
                    dve.wait_ge(summed, i * U + (U + u + 1))
                    dve.wait_ge(added, i * U + (u + 4))
                    acc = g["NUM"][:, ds(b, 1), :].rearrange("p a n -> p (a n)")
                    vec.tensor_tensor(acc, acc, sums[u % 4][:, 0:W], ALU.add).then_inc(added, 1)

            vec.memset(g["NUM"][:, :, :], 0.0).then_inc(added, 4)
            picks(0, 0)
            softmax(0, 0)
            picks(0, 1)
            with dve.Fori(0, NI // U) as i:
                for h in range(2):
                    messages(i, h)
                    softmax(*after(i, h))
                    adds(i, h)
                    picks(i + 1, h)


def stage_project(nc, sb, sem, g):
    t = norm_tiles(sb, sem, "ln4")
    xn, xt = sb("xp_xn", [P, GB, D]), sb("xp_xt", [P, 2, GN])
    w = sb("xp_w", [P, 2, 4 * D])
    b_ih, b_hh = sb("xp_bih", [P, 4 * D]), sb("xp_bhh", [P, 4 * D])
    out = sb("xp_out", [P, GB, 4 * D])
    den, att = sb("xp_den", [P, NB, HEADS]), sb("xp_att", [P, GB, D])
    loaded, trans, copied, whole, evac, step, stored, scaled = (sem("xp_" + n) for n in (
        "loaded", "trans", "copied", "whole", "evac", "step", "stored", "scaled"))
    ps = g["ps"]
    Q = 2 * GB
    with nc.Block() as block:
        @block.sync
        def _(sp):
            sp.dma_start(w[:, :, :], g["L1_ffn_W_ihT"].rearrange("(c p) n -> p c n", p=P)).then_inc(loaded, 16)
            sp.dma_start(b_ih[:, :], g["L1_ffn_b_ihP"].to_broadcast([P, 4 * D])).then_inc(loaded, 16)
            sp.dma_start(b_hh[:, :], g["L1_ffn_b_hhP"].to_broadcast([P, 4 * D])).then_inc(loaded, 16)
            with sp.Fori(0, NG) as i:
                sp.wait_ge(evac, i * Q + (Q + 4))
                sp.dma_start(g["xp"][ds(i * GN, GN), :].rearrange("(u p) n -> p u n", p=P), out[:, :, :]).then_inc(stored, 16)
            sp.wait_ge(stored, 16 * NG)

        @block.tensor
        def _(pe):
            pe.wait_ge(scaled, 6)
            with pe.Fori(0, NG) as i:
                pe.wait_ge(t["step"], i * LN_STEPS + LN_STEPS)
                transpose_group(pe, nc, xn, g["ident"], ps, trans)
                pe.wait_ge(copied, i * 4 + 4)
                for q in range(Q):
                    u, n = q // 2, q % 2
                    pe.wait_ge(evac, i * Q + (q + 1))
                    for c in range(2):
                        m = nc.tensor.matmul(ps[4 + q % 4][:, :], xt[:, c, u * P:(u + 1) * P], w[:, c, n * 512:(n + 1) * 512], start=c == 0, stop=c == 1)
                    m.then_inc(whole, 1)
                pe.wait_ge(evac, i * Q + (Q + 4))

        @block.scalar
        def _(act):
            with act.Fori(0, NG) as i:
                root_group(act, nc, t, i * LN_STEPS)
                copy_transposed(act, nc, ps, xt, trans, i * (2 * GB), copied)

        @block.vector
        def _(dve):
            vec = nc.vector
            vec.memset(out[:, 0, 0:1], 0.0).then_inc(evac, 4)
            dve.wait_ge(evac, 4)
            dve.wait_ge(loaded, 48)
            vec.tensor_tensor(b_ih[:, :], b_ih[:, :], b_hh[:, :], ALU.add).then_inc(step, 1)
            dve.wait_ge(step, 1)
            for row in (w[:, 0, :], w[:, 1, :], b_ih[:, :]):
                for a, b in ((0, 2 * HD), (3 * HD, 4 * HD)):
                    v = row.rearrange("p (j k) -> p j k", j=4)[:, :, a:b]
                    vec.tensor_scalar(v, v, 0.5, None, ALU.mult).then_inc(scaled, 1)
            dve.wait_ge(scaled, 6)
            dn = g["NUM"][:, 0:NB, D:D + HEADS]
            vec.tensor_scalar(den[:, :, :], dn, 0.0, None, ALU.is_equal).then_inc(step, 1)
            dve.wait_ge(step, 2)
            vec.tensor_tensor(den[:, :, :], den[:, :, :], dn, ALU.add).then_inc(step, 1)
            dve.wait_ge(step, 3)
            vec.reciprocal(den[:, :, :], den[:, :, :]).then_inc(step, 1)
            dve.wait_ge(step, 4)
            per = 2 * GB
            with dve.Fori(0, NG) as i:
                for u in range(GB):
                    vec.tensor_tensor(att[:, u, :].rearrange("p (h d) -> p h d", h=HEADS),
                                      g["NUM"][:, ds(i * GB + u, 1), 0:D].rearrange("p a (h d) -> p (a h) d", h=HEADS),
                                      den[:, ds(i * GB + u, 1), :].rearrange("p a h -> p h a").to_broadcast([P, HEADS, HD]), ALU.mult).then_inc(step, 1)
                dve.wait_ge(step, i * per + (4 + GB))
                for u in range(GB):
                    xb = g["X"][:, ds(i * GB + u, 1), :].rearrange("p a d -> p (a d)")
                    vec.tensor_tensor(xb, xb, att[:, u, :], ALU.add).then_inc(step, 1)
                dve.wait_ge(step, i * per + (4 + 2 * GB))
                own_wait(dve, g)
                layer_norm_group(dve, nc, g, lambda u: g["X"][:, ds(i * GB + u, 1), :], lambda u: xn[:, u, :], t, i * LN_STEPS, i)
                for q in range(Q):
                    dve.wait_ge(whole, i * Q + (q + 1))
                    vec.tensor_tensor(out[:, q // 2, (q % 2) * 512:(q % 2 + 1) * 512], ps[4 + q % 4][:, :],
                                      b_ih[:, (q % 2) * 512:(q % 2 + 1) * 512], ALU.add).then_inc(evac, 1)
                dve.wait_ge(stored, i * 16 + 16)


def stage_lstm(nc, sb, sem, g):
    w = sb("ls_w", [P, 2, 4, D])
    xp = sb("ls_xp", [P, 2, 4 * D])
    s = sb("ls_s", [P, 4 * HD])
    o = sb("ls_o", [P, HD])
    ab = sb("ls_ab", [P, 2 * HD])
    ht = sb("ls_ht", [P, LU, HD])
    free = sb("ls_free", [P, 1])
    ps = g["ps"]
    tc, h = ps[4][:, 0:HD], ps[5][:, 0:HD]
    A = 3 * HD
    w_loaded, zeroed, gates_ready, gates_done, ab_ready, c_ready, tc_ready, h_made, h_ready, kept, xp_used = (sem("ls_" + n) for n in (
        "w_loaded", "zeroed", "gates_ready", "gates_done", "ab_ready", "c_ready", "tc_ready", "h_made", "h_ready", "kept", "xp_used"))
    xp_in = [sem("ls_xp0"), sem("ls_xp1")]
    PER = 2 * LU
    KN = LU // KU
    with nc.Block() as block:
        @block.sync
        def _(sp):
            sp.dma_start(w[:, :, :, :].rearrange("p c j n -> p c (j n)"), g["L1_ffn_W_hhT"]).then_inc(w_loaded, 16)
            sp.wait_ge(zeroed, 1)
            for b in range(2):
                sp.dma_start(xp[0:LU, b, :], g["xp"][b * LU:(b + 1) * LU, :]).then_inc(xp_in[b], 16)
            with sp.Fori(0, N // PER - 1) as i:
                for b in range(2):
                    sp.wait_ge(xp_used, i * 2 + (b + 1))
                    sp.dma_start(xp[0:LU, b, :], g["xp"][ds((i * 2 + (b + 2)) * LU, LU), :]).then_inc(xp_in[b], 16)

        @block.gpsimd
        def _(pool):
            pool.memset(free[:, :], 0.0).then_inc(kept, KN)
            with pool.Fori(0, N // LU) as i:
                for q in range(KN):
                    pool.wait_ge(h_ready, i * LU + (KU * (q + 1) + 1))
                    nc.gpsimd.tensor_copy(g["HIST"][:, :, ds(i * LU + KU * q, KU)],
                                          ht[:, KU * q:KU * (q + 1), 0:33:32].rearrange("p u c -> p c u")).then_inc(kept, 1)

        @block.tensor
        def _(pe):
            pe.wait_ge(zeroed, 4)
            with pe.Fori(0, N // PER) as i:
                for b in range(2):
                    pe.wait_ge(xp_in[b], i * 16 + 16)
                    for u in range(LU):
                        k = b * LU + u
                        parts = ((ps[k % 2], 0, A), (ps[2 + k % 2], A, D))
                        for bank, lo, hi in parts:
                            for j in range(4):
                                m = nc.tensor.matmul(bank[32 * j:32 * j + 32, 0:hi - lo], g["ident"][:, u:u + 1].to_broadcast([P, 32]),
                                                     xp[:, b, j * D + lo:j * D + hi], start=True, stop=False, tile_position=(0, 32 * j))
                        if u == LU - 1:
                            m.then_inc(xp_used, 1)
                        pe.wait_ge(h_ready, i * PER + (k + 1))
                        for bank, lo, hi in parts:
                            for c in range(2):
                                for j in range(4):
                                    m = nc.tensor.matmul(bank[32 * j:32 * j + 32, 0:hi - lo], ht[:, (u - 1) % LU, 32 * c:32 * c + 32],
                                                         w[:, c, j, lo:hi], start=False, stop=c == 1, tile_position=(0, 32 * j))
                            m.then_inc(gates_ready, 1)

        @block.scalar
        def _(act):
            with act.Fori(0, N // PER) as i:
                for k in range(PER):
                    act.wait_ge(gates_ready, i * (2 * PER) + (2 * k + 1))
                    nc.scalar.activation(s[:, 0:A], ps[k % 2][:, 0:A], ACT.Tanh).then_inc(gates_done, 1)
                    act.wait_ge(gates_ready, i * (2 * PER) + (2 * k + 2))
                    nc.scalar.activation(o[:, :], ps[2 + k % 2][:, 0:HD], ACT.Tanh)
                    act.wait_ge(c_ready, i * PER + (k + 2))
                    nc.scalar.activation(tc, s[:, A:4 * HD], ACT.Tanh, scale=0.5).then_inc(tc_ready, 1)

        @block.vector
        def _(dve):
            vec = nc.vector
            vec.memset(xp[:, :, :], 0.0).then_inc(zeroed, 1)
            vec.memset(ht[:, :, :], 0.0).then_inc(h_ready, 1)
            vec.memset(s[:, A:4 * HD], 0.0).then_inc(c_ready, 1)
            dve.wait_ge(w_loaded, 16)
            for lo, hi, scale in ((0, 2 * HD, 0.25), (2 * HD, A, 0.5), (A, D, 0.25)):
                v = w[:, :, :, lo:hi].rearrange("p c j n -> p (c j) n")
                vec.tensor_scalar(v, v, scale, None, ALU.mult).then_inc(zeroed, 1)
            dve.wait_ge(c_ready, 1)
            dve.wait_ge(h_ready, 1)
            with dve.Fori(0, N // PER) as i:
                for k in range(PER):
                    n1, n2, u = i * PER + (k + 1), i * PER + (k + 2), k % LU
                    dve.wait_ge(gates_done, n1)
                    vec.scalar_tensor_tensor(out=ab[:, :], in0=s[:, 0:2 * HD], scalar=1.0, in1=s[:, 2 * HD:4 * HD],
                                             op0=ALU.add, op1=ALU.mult).then_inc(ab_ready, 1)
                    dve.wait_ge(ab_ready, n1)
                    vec.scalar_tensor_tensor(out=s[:, A:4 * HD], in0=ab[:, HD:2 * HD], scalar=0.5, in1=ab[:, 0:HD],
                                             op0=ALU.mult, op1=ALU.add).then_inc(c_ready, 1)
                    dve.wait_ge(tc_ready, n1)
                    vec.scalar_tensor_tensor(out=h, in0=o[:, :], scalar=1.0, in1=tc,
                                             op0=ALU.add, op1=ALU.mult).then_inc(h_made, 1)
                    dve.wait_ge(h_made, n1)
                    if u % KU == 0:
                        dve.wait_ge(kept, i * (2 * KN) + (k // KU + 1))
                    vec.transpose(ht[:, u, :], h).then_inc(h_ready, 1)


def stage_finish(nc, sb, sem, g):
    wl = sb("fi_wl", [P, 2, 2])
    bl = sb("fi_bl", [P, 2])
    fw, bw, nbw = sb("fi_fw", [P, 2]), sb("fi_bw", [P, 2]), sb("fi_nbw", [P, 2])
    gate = sb("fi_gate", [P, N])
    l0 = sb("fi_l0", [P, 2, 512])
    inc = sb("fi_inc", [P, N])
    tmp = sb("fi_tmp", [P, N])
    loaded, ready, logits, compared, step, turned, added, stored = (sem("fi_" + n) for n in (
        "loaded", "ready", "logits", "compared", "step", "turned", "added", "stored"))
    ps = g["ps"]
    hist = g["HIST"]
    chunks = [(a, min(512, N - a)) for a in range(0, N, 512)]
    with nc.Block() as block:
        @block.sync
        def _(sp):
            sp.dma_start(wl[:, :, :], g["L1_ffn_W_linT"]).then_inc(loaded, 16)
            sp.dma_start(bl[:, :], g["L1_ffn_b_lin"].to_broadcast([P, 2])).then_inc(loaded, 16)
            sp.dma_start(fw[:, :], g["L1_ffn_fw_attT"]).then_inc(loaded, 16)
            sp.dma_start(bw[:, :], g["L1_ffn_bw_attT"]).then_inc(loaded, 16)
            for q in range(NG):
                sp.wait_ge(added, min(NB, (q + 1) * GB))
                a, b = q * GB, min((q + 1) * GB, NB - 1)
                sp.dma_start(g["out"][a * P:b * P, :].rearrange("(b p) d -> p b d", p=P), g["X"][:, a:b, :]).then_inc(stored, 16)
            sp.dma_start(g["out"][(NB - 1) * P:N, :], g["X"][0:TAIL, NB - 1, :]).then_inc(stored, 16)
            sp.wait_ge(stored, 16 * (NG + 1))

        @block.tensor
        def _(pe):
            pe.wait_ge(ready, 3)
            for q, (a, n) in enumerate(chunks):
                if q >= 2:
                    pe.wait_ge(compared, 2 * (q - 1))
                for l in range(2):
                    for c in range(2):
                        m = nc.tensor.matmul(ps[2 * (q % 2) + l][:, 0:n], wl[:, c, l:l + 1].to_broadcast([P, P]), hist[:, c, a:a + n],
                                             start=c == 0, stop=c == 1)
                m.then_inc(logits, 1)
            pe.wait_ge(step, 2 * 6)
            for b in range(NB):
                rows = P if b < NB - 1 else TAIL
                if b >= 4:
                    pe.wait_ge(added, b - 3)
                for c in range(2):
                    m = nc.tensor.transpose(ps[4 + b % 4][0:rows, c * P:(c + 1) * P], hist[:, c, b * P:b * P + rows], g["ident"][:, :])
                m.then_inc(turned, 1)

        @block.vector
        def _(dve):
            vec = nc.vector
            n = [0]

            def link(ins):
                n[0] += 1
                ins.then_inc(step, 1)
                dve.wait_ge(step, n[0])

            dve.wait_ge(loaded, 64)
            vec.tensor_scalar(wl[:, :, :], wl[:, :, :], 0.5, None, ALU.mult).then_inc(ready, 1)
            vec.tensor_scalar(nbw[:, :], bw[:, :], -1.0, None, ALU.mult).then_inc(ready, 1)
            vec.memset(tmp[:, 0:1], 0.0).then_inc(ready, 1)
            dve.wait_ge(ready, 3)
            for q, (a, m) in enumerate(chunks):
                dve.wait_ge(logits, q + 1)
                if q >= 2:
                    dve.wait_ge(compared, 2 * (q - 1))
                vec.tensor_scalar(l0[:, q % 2, 0:m], ps[2 * (q % 2)][:, 0:m], bl[:, 0:1], None, ALU.add).then_inc(compared, 1)
                dve.wait_ge(compared, 2 * q + 1)
                vec.scalar_tensor_tensor(out=gate[:, a:a + m], in0=ps[2 * (q % 2) + 1][:, 0:m], scalar=bl[:, 1:2], in1=l0[:, q % 2, 0:m],
                                         op0=ALU.add, op1=ALU.is_gt).then_inc(compared, 1)
            dve.wait_ge(compared, 2 * len(chunks))
            for c in range(2):
                h = hist[:, c, :]
                link(vec.scalar_tensor_tensor(out=tmp[:, :], in0=h, scalar=0.5, in1=gate[:, :], op0=ALU.mult, op1=ALU.mult))
                link(vec.tensor_tensor_scan(inc[:, :], tmp[:, :], tmp[:, :], 0.0, ALU.add, ALU.bypass))
                link(vec.tensor_tensor(tmp[:, :], inc[:, :], tmp[:, :], ALU.subtract))
                link(vec.scalar_tensor_tensor(out=h, in0=tmp[:, :], scalar=fw[:, c:c + 1], in1=h, op0=ALU.mult, op1=ALU.add))
                link(vec.tensor_scalar(tmp[:, :], inc[:, :], inc[:, N - 1:N], None, ALU.subtract))
                link(vec.scalar_tensor_tensor(out=h, in0=tmp[:, :], scalar=nbw[:, c:c + 1], in1=h, op0=ALU.mult, op1=ALU.add))
            for b in range(NB):
                rows = P if b < NB - 1 else TAIL
                dve.wait_ge(turned, b + 1)
                x = g["X"][0:rows, b, :].rearrange("p (j c n) -> p c j n", j=4, c=2)
                vec.tensor_tensor(x, x, ps[4 + b % 4][0:rows, 0:D].rearrange("p (c j n) -> p c j n", c=2, j=4), ALU.add).then_inc(added, 1)


_INS = ["x", "src", "dst", "edge_weight", "L0_ffn_Wr", "L0_ffn_br", "L0_ffn_W1", "L0_ffn_b1T", "L0_ffn_W2", "L0_ffn_b2",
        "L0_ffn_gamma", "L0_ffn_beta", "L1_gnn_W_T", "L1_gnn_b", "L1_gnn_a_src", "L1_gnn_a_dst", "L1_ffn_W_ihT",
        "L1_ffn_W_hhT", "L1_ffn_b_ihP", "L1_ffn_b_hhP", "L1_ffn_W_linT", "L1_ffn_b_lin", "L1_ffn_fw_attT", "L1_ffn_bw_attT"]


def gate_order(w):
    import numpy as np
    w = np.asarray(w).reshape(4, 4, D // 4, -1)
    return np.ascontiguousarray(w.transpose(1, 0, 2, 3).reshape(4 * D, -1))


def unit_order(w):
    import numpy as np
    w = np.asarray(w)
    w = w.reshape(4, 2, 32, -1).transpose(0, 2, 1, 3).reshape(P, 2, -1)
    return np.ascontiguousarray(w)


def lay_out(i):
    import numpy as np
    i = {k: np.asarray(v) for k, v in i.items()}
    o = {k: i[k] for k in _INS if k in i}
    o["L0_ffn_b1T"] = np.ascontiguousarray(i["L0_ffn_b1"].reshape(NEXP, FC, P).transpose(2, 0, 1))
    o["L1_gnn_W_T"] = np.ascontiguousarray(i["L1_gnn_W"].T)
    o["L1_ffn_W_ihT"] = np.ascontiguousarray(gate_order(i["L1_ffn_W_ih"]).T)
    o["L1_ffn_W_hhT"] = unit_order(gate_order(i["L1_ffn_W_hh"]).T)
    o["L1_ffn_b_ihP"] = gate_order(i["L1_ffn_b_ih"]).reshape(1, -1)
    o["L1_ffn_b_hhP"] = gate_order(i["L1_ffn_b_hh"]).reshape(1, -1)
    o["L1_ffn_W_linT"] = unit_order(i["L1_ffn_W_lin"].T)
    o["L1_ffn_fw_attT"] = unit_order(i["L1_ffn_fw_att"].T).reshape(P, 2)
    o["L1_ffn_bw_attT"] = unit_order(i["L1_ffn_bw_att"].T).reshape(P, 2)
    o["L1_gnn_a_src"] = i["L1_gnn_a_src"].reshape(1, D)
    o["L1_gnn_a_dst"] = i["L1_gnn_a_dst"].reshape(1, D)
    o["L1_gnn_b"] = i["L1_gnn_b"].reshape(1, D)
    o["L1_ffn_b_lin"] = i["L1_ffn_b_lin"].reshape(1, 2)
    return o


def build(nc, ins, out):
    with ExitStack() as ctx:
        g = dict(ins)
        sem = lambda name: ctx.enter_context(nc.semaphore(name))
        keep = lambda name, shape, dt=F32: ctx.enter_context(nc.sbuf_tensor(name, shape, dt))
        g["ps"] = [ctx.enter_context(nc.psum_tensor(f"bank{k}", [P, 512], F32)) for k in range(8)]
        g["y"] = nc.dram_tensor("y_table", (NP, D), F32, kind="Internal").ap()
        g["rec"] = [nc.dram_tensor(f"rec_table{k}", (P * NI, RF), F32, kind="Internal").ap() for k in range(WAYS)]
        g["wh"] = nc.dram_tensor("wh_table", (NP, D), F32, kind="Internal").ap()
        g["ad"] = nc.dram_tensor("alpha_dst_table", (NP, HEADS), F32, kind="Internal").ap()
        g["xp"] = nc.dram_tensor("projections", (NP, 4 * D), F32, kind="Internal").ap()
        g["out"] = out
        g["waits_carried"] = {e: sem("waits_carried_" + e) for e in ("DVE", "Pool")}
        g["started"] = sem("started")
        g["scattered"] = [sem(f"scattered{k}") for k in range(WAYS)]
        g["got"] = [sem(f"got{u}") for u in range(U)]
        g["ident"] = keep("ident", [P, P])
        g["iota"] = keep("iota", [P, P])
        g["X"] = keep("X", [P, NB + 1, D])

        def stage(f):
            with ExitStack() as own:
                f(nc, lambda name, shape, dt=F32: own.enter_context(nc.sbuf_tensor(name, shape, dt)), sem, g)

        stage(stage_normalise)
        with ExitStack() as items:
            kept = lambda name, shape, dt=F32: items.enter_context(nc.sbuf_tensor(name, shape, dt))
            g["BW"] = kept("item_block", [P, NI])
            g["BI"] = kept("item_block_i", [1, NI + U], I32)
            with ExitStack() as recs:
                g["REC"] = recs.enter_context(nc.sbuf_tensor("records", [EP, EC, RF], F32))
                g["POS"] = recs.enter_context(nc.sbuf_tensor("places", [EP, EC], I32))
                stage(stage_places)
                stage(stage_scatter)
            g["DST"] = kept("item_dst", [P, NI + U], I32)
            g["LO"] = kept("item_lo", [P, NI + U])
            g["EW"] = kept("item_weight", [P, NI + U])
            stage(stage_items)
            stage(stage_aggregate)
            stage(stage_experts)
            g["AS"] = kept("alpha_src_and_max", [P, NB + 1, 2 * HEADS])
            stage(stage_heads)
            g["NUM"] = kept("numerators", [P, NB + 1, D + HEADS])
            with ExitStack() as scores:
                g["ADE"] = scores.enter_context(nc.sbuf_tensor("item_alpha_dst", [P, NI + U, HEADS], F32))
                stage(stage_maxima)
                stage(stage_attend)
            stage(stage_project)
        g["HIST"] = keep("history", [P, 2, N])
        stage(stage_lstm)
        stage(stage_finish)


def kernel(**inputs):
    from concourse import bacc
    from concourse.bass_utils import run_bass_kernel_spmd

    nc = bacc.Bacc("TRN2", target_bir_lowering=False, num_devices=1)
    arrays = lay_out(inputs)
    aps = {k: nc.dram_tensor("in_" + k, a.shape, mybir.dt.from_np(a.dtype), kind="ExternalInput").ap() for k, a in arrays.items()}
    out = nc.dram_tensor("out", (N, D), F32, kind="ExternalOutput").ap()
    build(nc, aps, out)
    r = run_bass_kernel_spmd(nc, [{"in_" + k: a for k, a in arrays.items()}], core_ids=[0])
    return r.results[0]["out"]
```

```python
from contextlib import ExitStack

import concourse.bass as bass
from concourse import mybir

F32 = mybir.dt.float32
BF16 = mybir.dt.bfloat16
I32 = mybir.dt.int32
ALU = mybir.AluOpType
ACT = mybir.ActivationFunctionType
AX = mybir.AxisListType
ds = bass.ds

P = 128
N = 6250
D = 256
E = 200000
NB = -(-N // P)
NP = NB * P
TAIL = N - (NB - 1) * P
GB = 7
NG = NB // GB
GN = GB * P
HEADS = 4
HD = D // HEADS
EP = 125
EC = E // EP
U = 16
HU = U // 2
GU = 4
GPT = U // GU
UP = U // 2
NI = -(-((E - NB) // (2 * P) + NB) // UP) * U
TURNS = NI // U
RF = 3
SU = 20
WAYS = 5
BIG = 3.0e38
EPS = 1e-5
NEXP, FF = 8, 512
FC = FF // P
CAP = float(-(-N * 5 // (4 * NEXP)))
LU = 25
KU = 5


def own_wait(eng, g):
    eng.sem_inc(g["waits_carried"][eng.engine.name], 1)


def pair_blocks(nc, g, engine, i, k0, n):
    return nc.values_load_multi_w_load_instructions(
        g["BI"][0:1, ds(i * UP + k0, n)], [engine], min_val=0, max_val=NB,
        skip_runtime_bounds_check_because="a number of blocks counted on the chip, at most NB")[1]


def layer_norm_group(dve, nc, g, rows, out, t, base, i):
    step, mv, root, rstd, tmp = t["step"], t["mv"], t["root"], t["rstd"], t["tmp"]
    n = [0]

    def done(ins):
        n[0] += 1
        ins.then_inc(step, 1)

    def reads_last():
        dve.wait_ge(step, base + n[0])

    for u in range(GB):
        done(nc.vector.bn_stats(t["stats"][:, u, :], rows(u)))
    reads_last()
    own_wait(dve, g)
    for u in range(GB):
        done(nc.vector.bn_aggr(mv[:, u, :], t["stats"][:, u, :]))
    reads_last()
    done(nc.vector.tensor_scalar(t["ve"][:, :], mv[:, :, 1], EPS, None, ALU.add))
    dve.wait_ge(t["rooted"], i + 1)
    done(nc.vector.reciprocal(rstd[:, :], root[:, :]))
    reads_last()
    done(nc.vector.tensor_tensor(tmp[:, :], t["ve"][:, :], rstd[:, :], ALU.mult))
    reads_last()
    done(nc.vector.tensor_tensor(tmp[:, :], tmp[:, :], rstd[:, :], ALU.mult))
    reads_last()
    done(nc.vector.tensor_scalar(tmp[:, :], tmp[:, :], -0.5, 1.5, ALU.mult, ALU.add))
    reads_last()
    done(nc.vector.tensor_tensor(rstd[:, :], rstd[:, :], tmp[:, :], ALU.mult))
    reads_last()
    for u in range(GB):
        done(nc.vector.tensor_scalar(out(u), rows(u), mv[:, u, 0:1], rstd[:, u:u + 1], ALU.subtract, ALU.mult))


LN_STEPS = 3 * GB + 6
LN_VE = 2 * GB + 1


def root_group(act, nc, t, base):
    act.wait_ge(t["step"], base + LN_VE)
    nc.scalar.sqrt(t["root"][:, :], t["ve"][:, :]).then_inc(t["rooted"], 1)


def norm_tiles(sb, sem, tag):
    small = {k: sb(f"{tag}_{k}", [P, GB]) for k in ("ve", "root", "rstd", "tmp")}
    return {"rooted": sem(tag + "_rooted"), "step": sem(tag + "_step"), "stats": sb(tag + "_stats", [P, GB, 6]),
            "mv": sb(tag + "_mv", [P, GB, 2])} | small


def transpose_group(pe, nc, src, ident, tps, done):
    for c in range(2):
        for u in range(GB):
            nc.tensor.transpose(tps[2 * c + u // 4][:, (u % 4) * P:(u % 4 + 1) * P],
                                src[:, u, c * P:(c + 1) * P], ident[:, :]).then_inc(done, 1)


def copy_transposed(act, nc, tps, xt, done, base, copied):
    for c in range(2):
        for h, (a, n) in enumerate(((0, 4), (4, GB - 4))):
            act.wait_ge(done, base + c * GB + a + n)
            nc.scalar.copy(xt[:, c, a * P:(a + n) * P], tps[2 * c + h][:, 0:n * P]).then_inc(copied, 1)


def stage_normalise(nc, sb, sem, g):
    t = norm_tiles(sb, sem, "ln0")
    yt = sb("ln0_out", [P, GB, D])
    x_loaded, pads, step, stored, made = sem("x_loaded"), g["started"], t["step"], sem("y_stored"), sem("consts_made")
    with nc.Block() as block:
        @block.sync
        def _(sp):
            sp.wait_ge(pads, 1)
            sp.dma_start(g["X"][:, 0:NB - 1, :], g["x"][0:(NB - 1) * P, :].rearrange("(b p) d -> p b d", p=P)).then_inc(x_loaded, 16)
            sp.dma_start(g["X"][0:TAIL, NB - 1, :], g["x"][(NB - 1) * P:N, :]).then_inc(x_loaded, 16)
            with sp.Fori(0, NG) as i:
                sp.wait_ge(step, i * LN_STEPS + LN_STEPS)
                sp.dma_start(g["y"][ds(i * GN, GN), :].rearrange("(u p) d -> p u d", p=P), yt[:, :, :]).then_inc(stored, 16)
            sp.wait_ge(stored, 16 * NG + 16)

        @block.gpsimd
        def _(pool):
            pool.memset(g["ident"][:, :], 0.0).then_inc(made, 1)
            pool.iota(g["iota"][:, :], [[1, P]], base=0, channel_multiplier=0, allow_small_or_imprecise_dtypes=True).then_inc(made, 1)
            pool.memset(yt[:, 0, 0:1], 0.0).then_inc(stored, 16)
            pool.wait_ge(made, 2)
            pool.affine_select(out=g["ident"][:, :], in_=g["ident"][:, :], compare_op=ALU.not_equal, fill=1.0,
                               base=0, pattern=[[-1, P]], channel_multiplier=1).then_inc(made, 1)
            pool.wait_ge(made, 3)

        @block.scalar
        def _(act):
            with act.Fori(0, NG) as i:
                root_group(act, nc, t, i * LN_STEPS)

        @block.vector
        def _(dve):
            nc.vector.memset(g["X"][:, NB - 1:NB + 1, :], 0.0).then_inc(pads, 1)
            dve.wait_ge(pads, 1)
            dve.wait_ge(x_loaded, 32)
            with dve.Fori(0, NG) as i:
                dve.wait_ge(stored, i * 16 + 16)
                own_wait(dve, g)
                layer_norm_group(dve, nc, g, lambda u: g["X"][:, ds(i * GB + u, 1), :], lambda u: yt[:, u, :], t, i * LN_STEPS, i)


def stage_places(nc, sb, sem, g):
    src = sb("src_i", [EP, EC], I32)
    hi_i = sb("hi_i", [EP, EC], I32)
    hi = sb("hi", [EP, EC])
    dst = sb("dst_i", [EP, EC], I32)
    ew = sb("ew_in", [EP, EC])
    in_b = sb("in_b", [EP, EC], I32)
    rank = sb("rank", [EP, EC])
    pos = sb("pos", [EP, EC])
    pos_i = sb("pos_i", [EP, EC], I32)
    col_i = sb("col_i", [EP, EC], I32)
    zero = sb("zero", [P, NI * RF])
    upper = sb("upper", [P, P])
    ones = sb("ones_c", [P, P])
    cnt = sb("cnt", [EP, NB])
    tot = sb("tot", [P, NB])
    tot_i = sb("tot_i", [P, NB], I32)
    nit = sb("nit", [P, NB])
    cum = sb("cum", [P, NB])
    first = sb("first", [EP, NB])
    off = sb("off", [EP, NB])
    item = sb("item", [P, NI])
    counts_ps = g["ps"][0]
    loaded, ready, step, counted, summed, s_item, s_bw, s_bw2 = (sem(n) for n in (
        "edges_loaded", "sort_consts", "sort_step", "bucket_counted", "bucket_summed", "item_step", "s_bw", "s_bw2"))
    with nc.Block() as block:
        @block.sync
        def _(sp):
            sp.dma_start(src[:, :], g["src"].rearrange("(p c) -> p c", p=EP)).then_inc(loaded, 16)
            sp.dma_start(dst[:, :], g["dst"].rearrange("(p c) -> p c", p=EP)).then_inc(loaded, 16)
            sp.dma_start(ew[:, :], g["edge_weight"].rearrange("(p c) -> p c", p=EP)).then_inc(loaded, 16)

        @block.gpsimd
        def _(pool):
            pool.memset(zero[:, :], 0.0).then_inc(ready, 1)
            pool.memset(ones[:, :], 1.0).then_inc(ready, 1)
            pool.memset(upper[:, :], 1.0).then_inc(ready, 1)
            pool.iota(item[:, :], [[1, NI]], base=0, channel_multiplier=0, allow_small_or_imprecise_dtypes=True).then_inc(ready, 1)
            pool.wait_ge(ready, 4)
            for k in range(WAYS):
                pool.dma_start(g["rec"][k].rearrange("(p r) f -> p (r f)", p=P), zero[:, :]).then_inc(g["scattered"][k], 16)
            pool.affine_select(out=upper[:, :], in_=upper[:, :], compare_op=ALU.is_gt, fill=0.0, base=0,
                               pattern=[[1, P]], channel_multiplier=-1).then_inc(ready, 1)
            for k in range(WAYS):
                pool.wait_ge(g["scattered"][k], 16)

        @block.tensor
        def _(pe):
            pe.wait_ge(ready, 5)
            pe.wait_ge(counted, NB)
            nc.tensor.matmul(counts_ps[0:EP, 0:NB], upper[0:EP, 0:EP], cnt[:, :], start=True, stop=True)
            nc.tensor.matmul(g["ps"][1][:, 0:NB], ones[0:EP, :], cnt[:, :], start=True, stop=True).then_inc(summed, 1)

        @block.vector
        def _(dve):
            n = [0]

            def link(ins):
                n[0] += 1
                ins.then_inc(step, 1)
                dve.wait_ge(step, n[0])

            dve.wait_ge(loaded, 48)
            link(nc.vector.tensor_single_scalar(hi_i[:, :], src[:, :], 7, ALU.arith_shift_right))
            link(nc.vector.tensor_copy(hi[:, :], hi_i[:, :]))
            link(nc.vector.tensor_scalar(g["REC"][:, :, 0], src[:, :], 1.0, None, ALU.add))
            link(nc.vector.tensor_copy(g["REC"][:, :, 1], dst[:, :]))
            link(nc.vector.tensor_copy(g["REC"][:, :, 2], ew[:, :]))
            dve.wait_ge(ready, 5)
            with dve.Fori(0, NB) as b:
                nc.vector.tensor_scalar(rank[:, :], hi[:, :], item[0:EP, ds(b, 1)], 0.0, ALU.is_equal, ALU.add,
                                        accum_out=cnt[:, ds(b, 1)]).then_inc(counted, 1)
                dve.wait_ge(counted, b + 1)
            dve.wait_ge(summed, 1)
            link(nc.vector.tensor_copy(tot[:, :], g["ps"][1][:, 0:NB]))
            link(nc.vector.tensor_scalar(tot_i[:, :], tot[:, :], float(2 * P - 1), None, ALU.add))
            link(nc.vector.tensor_single_scalar(tot_i[:, :], tot_i[:, :], 8, ALU.arith_shift_right))
            link(nc.vector.tensor_scalar(nit[:, :], tot_i[:, :], 2.0, None, ALU.mult))
            link(nc.vector.tensor_tensor_scan(cum[:, :], nit[:, :], nit[:, :], 0.0, ALU.add, ALU.bypass))
            link(nc.vector.tensor_tensor(first[:, :], cum[0:EP, :], nit[0:EP, :], ALU.subtract))
            link(nc.vector.tensor_scalar(first[:, :], first[:, :], float(P), -1.0, ALU.mult, ALU.add))
            link(nc.vector.tensor_tensor(off[:, :], first[:, :], counts_ps[0:EP, 0:NB], ALU.add))
            link(nc.vector.memset(g["BW"][:, :], 0.0))
            m0 = n[0]
            with dve.Fori(0, NB) as b:
                nc.vector.tensor_single_scalar(in_b[:, :], hi[:, :], item[0:EP, ds(b, 1)], ALU.is_equal).then_inc(s_item, 1)
                dve.wait_ge(s_item, b * 3 + 1)
                nc.vector.tensor_tensor_scan(rank[:, :], in_b[:, :], in_b[:, :], off[:, ds(b, 1)], ALU.add, ALU.bypass).then_inc(s_item, 1)
                nc.vector.scalar_tensor_tensor(out=g["BW"][:, :], in0=item[:, :], scalar=cum[:, ds(b, 1)], in1=g["BW"][:, :],
                                               op0=ALU.is_ge, op1=ALU.add).then_inc(s_bw, 1)
                dve.wait_ge(s_item, b * 3 + 2)
                own_wait(dve, g)
                nc.vector.copy_predicated(pos[:, :], in_b[:, :], rank[:, :]).then_inc(s_item, 1)
                dve.wait_ge(s_item, b * 3 + 3)
                dve.wait_ge(s_bw, b + 1)
            link(nc.vector.tensor_copy(pos_i[:, :], pos[:, :]))
            link(nc.vector.tensor_single_scalar(col_i[:, :], pos_i[:, :], 7, ALU.arith_shift_right))
            link(nc.vector.tensor_single_scalar(pos_i[:, :], pos_i[:, :], P - 1, ALU.bitwise_and))
            link(nc.vector.scalar_tensor_tensor(out=g["POS"][:, :], in0=pos_i[:, :], scalar=float(NI), in1=col_i[:, :],
                                                op0=ALU.mult, op1=ALU.add))


def stage_scatter(nc, sb, sem, g):
    SH = SU // 2
    per = SU // WAYS
    recs = sb("st_rec", [EP, 2, SH, RF])
    idx = sb("st_idx", [EP, 2, SH], I32)
    staged = sem("scatter_staged")
    with nc.Block() as block:
        @block.scalar
        def _(act):
            def stage_half(i, h):
                nc.scalar.copy(recs[:, h, :, :], g["REC"][:, ds(i * SU + h * SH, SH), :]).then_inc(staged, 1)
                nc.scalar.copy(idx[:, h, :], g["POS"][:, ds(i * SU + h * SH, SH)]).then_inc(staged, 1)

            stage_half(0, 0)
            stage_half(0, 1)
            with act.Fori(0, EC // SU - 1) as i:
                for h in range(2):
                    for k in range(WAYS):
                        act.wait_ge(g["scattered"][k], i * (16 * per) + 16 * (1 + (h + 1) * per // 2))
                    stage_half(i + 1, h)

        @block.gpsimd
        def _(pool):
            with pool.Fori(0, EC // SU) as i:
                for u in range(SU):
                    h, k, turn = u // SH, u % WAYS, u // WAYS
                    if u % SH == 0:
                        pool.wait_ge(staged, i * 4 + (2 * h + 2))
                    pool.wait_ge(g["scattered"][k], i * (16 * per) + 16 * (1 + turn))
                    own_wait(pool, g)
                    pool.indirect_dma_start(g["rec"][k], bass.IndirectOffsetOnAxis(ap=idx[:, h, u % SH:u % SH + 1], axis=0),
                                            recs[:, h, u % SH, :], None).then_inc(g["scattered"][k], 16)
            for k in range(WAYS):
                pool.wait_ge(g["scattered"][k], 16 * (1 + EC // WAYS))


def stage_items(nc, sb, sem, g):
    part = [sb(f"rec_part{k}", [P, NI * RF]) for k in range(WAYS)]
    loaded, step = sem("rec_loaded"), sem("items_step")
    with nc.Block() as block:
        @block.sync
        def _(sp):
            for k in range(WAYS):
                sp.dma_start(part[k][:, :], g["rec"][k].rearrange("(p r) f -> p (r f)", p=P)).then_inc(loaded, 16)

        @block.vector
        def _(dve):
            n = [0]

            def link(ins):
                n[0] += 1
                ins.then_inc(step, 1)
                dve.wait_ge(step, n[0])

            dve.wait_ge(loaded, 16 * WAYS)
            for k in range(1, WAYS):
                link(nc.vector.tensor_tensor(part[0][:, :], part[0][:, :], part[k][:, :], ALU.add))
            rec = part[0][:, :].rearrange("p (r f) -> p r f", f=RF)
            link(nc.vector.tensor_copy(g["DST"][:, 0:NI], rec[:, :, 1]))
            link(nc.vector.tensor_copy(g["EW"][:, 0:NI], rec[:, :, 2]))
            link(nc.vector.tensor_scalar(part[1][:, 0:NI], g["BW"][:, :], float(P), 1.0, ALU.mult, ALU.add))
            link(nc.vector.tensor_tensor(g["LO"][:, 0:NI], rec[:, :, 0], part[1][:, 0:NI], ALU.subtract))
            link(nc.vector.tensor_copy(g["BI"][0:1, 0:NI // 2], g["BW"][0:1, 0:NI:2]))
            link(nc.vector.memset(g["BI"][0:1, NI // 2:NI // 2 + UP], NB))
            link(nc.vector.memset(g["DST"][:, NI:NI + U], 0))
            link(nc.vector.memset(g["LO"][:, NI:NI + U], -1.0))
            link(nc.vector.memset(g["EW"][:, NI:NI + U], 0.0))


def gather_rows(pool, nc, g, table, rows, idx, staged, summed):
    with pool.Fori(0, TURNS) as i:
        for q in range(GPT):
            if q % 2 == 0:
                pool.wait_ge(staged, i * 2 + (q // 2 + 1))
            pool.wait_ge(summed, i * UP + 2 * (q + 1))
            own_wait(pool, g)
            for u in range(q * GU, (q + 1) * GU):
                pool.indirect_dma_start(rows[:, u, :], None, table,
                                        bass.IndirectOffsetOnAxis(ap=idx[:, u // HU, u % HU:u % HU + 1], axis=0)).then_inc(g["got"][q], 16)


def stage_indices(nc, g, idx, i, h, staged):
    nc.scalar.copy(idx[:, h, :], g["DST"][:, ds(i * U + h * HU, HU)]).then_inc(staged, 1)


def one_hots(nc, g, pick, i, u, n):
    return nc.vector.tensor_tensor(pick[:, u:u + n, :], g["iota"][:, :].rearrange("p (a e) -> p a e", a=1).to_broadcast([P, n, P]),
                                   g["LO"][:, ds(i * U + u, n)].rearrange("p (u a) -> p u a", a=1).to_broadcast([P, n, P]), ALU.is_equal)


def stage_aggregate(nc, sb, sem, g):
    idx = sb("ag_idx", [P, 2, HU], I32)
    rows = sb("ag_rows", [P, U, D])
    pick = sb("ag_pick", [P, U, P])
    free = sb("ag_free", [1, 2])
    sums = [g["ps"][k][:, 0:D] for k in range(UP)]
    staged, picked, summed, added = (sem(n) for n in ("ag_staged", "ag_picked", "ag_summed", "ag_added"))
    with nc.Block() as block:
        @block.scalar
        def _(act):
            for h in range(2):
                stage_indices(nc, g, idx, 0, h, staged)
            with act.Fori(0, TURNS) as i:
                for h in range(2):
                    for q in (2 * h, 2 * h + 1):
                        act.wait_ge(g["got"][q], i * (16 * GU) + 16 * GU)
                    stage_indices(nc, g, idx, i + 1, h, staged)

        @block.gpsimd
        def _(pool):
            pool.memset(free[:, 0:1], 0.0).then_inc(summed, UP)
            gather_rows(pool, nc, g, g["y"], rows, idx, staged, summed)

        @block.tensor
        def _(pe):
            with pe.Fori(0, TURNS) as i:
                for k in range(UP):
                    pe.wait_ge(picked, i * UP + (k + 1))
                    pe.wait_ge(added, i * UP + (k + 1))
                    if k % 2 == 0:
                        pe.wait_ge(g["got"][k // 2], i * (16 * GU) + 16 * GU)
                    for u in (2 * k, 2 * k + 1):
                        m = nc.tensor.matmul(sums[k], pick[:, u, :], rows[:, u, :], start=u == 2 * k, stop=u == 2 * k + 1)
                    m.then_inc(summed, 1)

        @block.vector
        def _(dve):
            def picks(i, h):
                dve.wait_ge(summed, i * UP + (h + 1) * (UP // 2))
                for u in range(h * HU, (h + 1) * HU):
                    m = nc.vector.tensor_scalar(pick[:, u, :], g["iota"][:, :], g["LO"][:, ds(i * U + u, 1)], g["EW"][:, ds(i * U + u, 1)],
                                                ALU.is_equal, ALU.mult)
                    if u % 2 == 1:
                        m.then_inc(picked, 1)

            def adds(i, h):
                blocks = pair_blocks(nc, g, mybir.EngineType.DVE, i, h * UP // 2, UP // 2)
                for n, b in enumerate(blocks):
                    k = h * UP // 2 + n
                    dve.wait_ge(summed, i * UP + (UP + k + 1))
                    dve.wait_ge(added, i * UP + (UP + k))
                    nc.vector.tensor_tensor(g["X"][:, ds(b, 1), :], g["X"][:, ds(b, 1), :], sums[k], ALU.add).then_inc(added, 1)

            nc.vector.memset(free[:, 1:2], 0.0).then_inc(added, UP)
            picks(0, 0)
            with dve.Fori(0, TURNS) as i:
                picks(i, 1)
                adds(i, 0)
                picks(i + 1, 0)
                adds(i, 1)


def stage_experts(nc, sb, sem, g):
    t = norm_tiles(sb, sem, "ln1")
    t2 = norm_tiles(sb, sem, "ln2")
    xn = sb("moe_xn", [P, NB, D])
    xt = sb("moe_xt", [P, 2, GN])
    hid = sb("moe_hid", [P, 2 * FC, GN])
    w1 = sb("moe_w1", [P, 2, 2, FF])
    w2 = sb("moe_w2", [P, 2, FC, D])
    b1 = sb("moe_b1", [P, 2, FC])
    b2 = sb("moe_b2", [P, 2, D])
    gam, bet = sb("moe_gamma", [P, D]), sb("moe_beta", [P, D])
    wr = sb("moe_wr", [P, 2, NEXP])
    row = {k: sb("moe_" + k, [1, NEXP]) for k in ("br", "lg", "ex", "rw", "sc", "el", "eq", "io", "cd", "rw2")}
    sc1 = {k: sb("moe1_" + k, [1, 1]) for k in ("mx", "sm", "rc")}
    top, idx_f, idx_i = sb("moe_top", [1, 2]), sb("moe_idxf", [1, 2]), sb("moe_idxi", [1, 2], I32)
    wts, wb = sb("moe_wts", [1, 2]), sb("moe_wb", [P, 2])
    mrow, mcol, ones, onef = sb("moe_mrow", [1, D]), sb("moe_mcol", [P, 2]), sb("moe_ones", [P, 1]), sb("moe_onesr", [1, P])
    v, nv = sb("moe_v", [P, GB, D]), sb("moe_nv", [P, GB, D])
    small, big, made, meant, mean_c, meanT, mcopied, logit, exp_in, exp_out = (sem("moe_" + n) for n in (
        "small", "big", "made", "meant", "mean_c", "meanT", "mcopied", "logit", "exp_in", "exp_out"))
    route, weighted, spread, trans, copied, h_ready, gelud, o_ready, evac, fin = (sem("moe_" + n) for n in (
        "route", "weighted", "spread", "trans", "copied", "h_ready", "gelud", "o_ready", "evac", "fin"))
    picked, scaled, v_ready = sem("moe_picked"), sem("moe_scaled"), sem("moe_v_ready")
    step = sem("moe_step")
    ps = g["ps"]
    half = GN // 2
    with nc.Block() as block:
        @block.sync
        def _(sp):
            sp.dma_start(wr[:, :, :], g["L0_ffn_Wr"].rearrange("(c p) e -> p c e", p=P)).then_inc(small, 16)
            sp.dma_start(row["br"][:, :], g["L0_ffn_br"].rearrange("(a e) -> a e", a=1)).then_inc(small, 16)
            sp.dma_start(gam[:, :], g["L0_ffn_gamma"].rearrange("(a e) -> a e", a=1).to_broadcast([P, D])).then_inc(small, 16)
            sp.dma_start(bet[:, :], g["L0_ffn_beta"].rearrange("(a e) -> a e", a=1).to_broadcast([P, D])).then_inc(small, 16)
            sp.wait_ge(picked, 1)
            for k in range(2):
                e = nc.sync.value_load(idx_i[0:1, k:k + 1], min_val=0, max_val=NEXP - 1)
                sp.dma_start(w1[:, k, :, :], g["L0_ffn_W1"][ds(e, 1), :, :].rearrange("a (c p) f -> p (a c) f", p=P)).then_inc(big, 16)
                sp.dma_start(w2[:, k, :, :], g["L0_ffn_W2"][ds(e, 1), :, :].rearrange("a (c p) d -> p (a c) d", p=P)).then_inc(big, 16)
                sp.dma_start(b1[:, k, :], g["L0_ffn_b1T"][:, ds(e, 1), :].rearrange("p a c -> p (a c)")).then_inc(big, 16)
                sp.dma_start(b2[:, k, :], g["L0_ffn_b2"][ds(e, 1), :].to_broadcast([P, D])).then_inc(big, 16)

        @block.gpsimd
        def _(pool):
            pool.memset(ones[:, :], 1.0).then_inc(made, 1)
            pool.memset(onef[:, :], 1.0).then_inc(made, 1)
            pool.iota(row["io"][:, :], [[1, NEXP]], base=0, channel_multiplier=0, allow_small_or_imprecise_dtypes=True).then_inc(made, 1)
            pool.memset(v[:, :, :], 0.0).then_inc(trans, 2 * GB)
            pool.wait_ge(t["step"], NG * LN_STEPS)
            with pool.Fori(0, NG) as i:
                pool.wait_ge(trans, i * (2 * GB) + 2 * GB)
                nc.gpsimd.tensor_copy(v[:, :, :], xn[:, ds(i * GB, GB), :]).then_inc(v_ready, 1)

        @block.tensor
        def _(pe):
            pe.wait_ge(made, 3)
            pe.wait_ge(t["step"], NG * LN_STEPS)
            nc.tensor.matmul(ps[0][0:1, 0:D], ones[:, 0:1], xn[:, 0, :], start=True, stop=False)
            with pe.Fori(1, NB - 1) as b:
                nc.tensor.matmul(ps[0][0:1, 0:D], ones[:, 0:1], xn[:, ds(b, 1), :], start=False, stop=False)
            nc.tensor.matmul(ps[0][0:1, 0:D], ones[0:TAIL, 0:1], xn[0:TAIL, NB - 1, :], start=False, stop=True).then_inc(meant, 1)
            pe.wait_ge(mean_c, 1)
            for c in range(2):
                nc.tensor.matmul(ps[1][:, c:c + 1], mrow[0:1, c * P:(c + 1) * P], onef[0:1, 0:1], start=True, stop=True).then_inc(meanT, 1)
            pe.wait_ge(mcopied, 1)
            pe.wait_ge(small, 64)
            for c in range(2):
                nc.tensor.matmul(ps[2][0:1, 0:NEXP], mcol[:, c:c + 1], wr[:, c, :], start=c == 0, stop=c == 1).then_inc(logit, 1)
            pe.wait_ge(weighted, 1)
            nc.tensor.matmul(ps[3][:, 0:2], onef[0:1, :], wts[0:1, :], start=True, stop=True).then_inc(spread, 1)
            pe.wait_ge(scaled, 1)
            with pe.Fori(0, NG) as i:
                pe.wait_ge(v_ready, i + 1)
                transpose_group(pe, nc, v, g["ident"], ps, trans)
                pe.wait_ge(copied, i * 4 + 4)
                for q in range(4 * FC):
                    k, s, f = q // (2 * FC), q // FC % 2, q % FC
                    pe.wait_ge(gelud, i * (4 * FC) + (q + 1))
                    for c in range(2):
                        m = nc.tensor.matmul(ps[4 + q % 2][:, 0:half], w1[:, k, c, f * P:(f + 1) * P], xt[:, c, s * half:(s + 1) * half],
                                             start=c == 0, stop=c == 1)
                    m.then_inc(h_ready, 1)
                pe.wait_ge(gelud, i * (4 * FC) + (4 * FC + 2))
                for u in range(GB):
                    pe.wait_ge(evac, i * GB + (u + 1))
                    for q in range(2 * FC):
                        m = nc.tensor.matmul(ps[6 + u % 2][:, 0:D], hid[:, q, u * P:(u + 1) * P], w2[:, q // FC, q % FC, :],
                                             start=q == 0, stop=q == 2 * FC - 1)
                    m.then_inc(o_ready, 1)

        @block.scalar
        def _(act):
            with act.Fori(0, NG) as i:
                root_group(act, nc, t, i * LN_STEPS)
            act.wait_ge(meant, 1)
            nc.scalar.mul(mrow[:, :], ps[0][0:1, 0:D], 1.0 / N).then_inc(mean_c, 1)
            act.wait_ge(meanT, 2)
            nc.scalar.copy(mcol[:, :], ps[1][:, 0:2]).then_inc(mcopied, 1)
            for n in range(2):
                act.wait_ge(exp_in, n + 1)
                nc.scalar.activation(row["ex"][:, :], row["sc"][:, :], ACT.Exp).then_inc(exp_out, 1)
            act.wait_ge(exp_in, 3)
            nc.scalar.activation(wts[:, :], top[:, :], ACT.Exp).then_inc(exp_out, 1)
            act.wait_ge(big, 16 * 8)
            with act.Fori(0, NG) as i:
                copy_transposed(act, nc, ps, xt, trans, i * (2 * GB) + 2 * GB, copied)
                for q in range(4 * FC):
                    k, s, f = q // (2 * FC), q // FC % 2, q % FC
                    act.wait_ge(h_ready, i * (4 * FC) + (q + 1))
                    nc.scalar.activation(hid[:, k * FC + f, s * half:(s + 1) * half], ps[4 + q % 2][:, 0:half], ACT.Gelu,
                                         bias=b1[:, k, f:f + 1]).then_inc(gelud, 1)
                root_group(act, nc, t2, i * LN_STEPS)

        @block.vector
        def _(dve):
            n = [0]

            def link(ins):
                n[0] += 1
                ins.then_inc(step, 1)
                dve.wait_ge(step, n[0])

            with dve.Fori(0, NG) as i:
                layer_norm_group(dve, nc, g, lambda u: g["X"][:, ds(i * GB + u, 1), :], lambda u: xn[:, ds(i * GB + u, 1), :], t, i * LN_STEPS, i)
            vec = nc.vector
            r = row
            dve.wait_ge(logit, 2)
            dve.wait_ge(small, 64)
            dve.wait_ge(made, 3)
            link(vec.tensor_tensor(r["lg"][:, :], ps[2][0:1, 0:NEXP], r["br"][:, :], ALU.add))

            def softmax(src, dst, turn):
                link(vec.tensor_reduce(sc1["mx"][:, :], src[:, :], AX.X, ALU.max))
                vec.tensor_scalar(r["sc"][:, :], src[:, :], sc1["mx"][:, 0:1], None, ALU.subtract).then_inc(exp_in, 1)
                dve.wait_ge(exp_out, turn)
                link(vec.tensor_reduce(sc1["sm"][:, :], r["ex"][:, :], AX.X, ALU.add))
                link(vec.reciprocal(sc1["rc"][:, :], sc1["sm"][:, :]))
                link(vec.tensor_scalar(dst[:, :], r["ex"][:, :], sc1["rc"][:, 0:1], None, ALU.mult))

            softmax(r["lg"], r["rw"], 1)
            link(vec.tensor_scalar(r["el"][:, :], r["rw"][:, :], float(N), None, ALU.mult))
            link(vec.tensor_scalar(r["cd"][:, :], r["el"][:, :], CAP, None, ALU.max))
            link(vec.reciprocal(r["eq"][:, :], r["cd"][:, :]))
            link(vec.tensor_scalar(r["eq"][:, :], r["eq"][:, :], CAP, -1.0, ALU.mult, ALU.add))
            link(vec.tensor_scalar(r["cd"][:, :], r["el"][:, :], CAP, None, ALU.is_gt))
            link(vec.tensor_tensor(r["eq"][:, :], r["eq"][:, :], r["cd"][:, :], ALU.mult))
            link(vec.tensor_scalar(r["eq"][:, :], r["eq"][:, :], 1.0, None, ALU.add))
            link(vec.tensor_tensor(r["rw"][:, :], r["rw"][:, :], r["eq"][:, :], ALU.mult))
            softmax(r["rw"], r["rw2"], 2)
            for k in range(2):
                link(vec.tensor_reduce(top[:, k:k + 1], r["rw2"][:, :], AX.X, ALU.max))
                link(vec.tensor_scalar(r["eq"][:, :], r["rw2"][:, :], top[:, k:k + 1], float(NEXP), ALU.is_lt, ALU.mult))
                link(vec.tensor_tensor(r["cd"][:, :], r["eq"][:, :], r["io"][:, :], ALU.add))
                link(vec.tensor_reduce(idx_f[:, k:k + 1], r["cd"][:, :], AX.X, ALU.min))
                link(vec.tensor_scalar(r["eq"][:, :], r["io"][:, :], idx_f[:, k:k + 1], -4.0, ALU.is_equal, ALU.mult))
                link(vec.tensor_tensor(r["rw2"][:, :], r["rw2"][:, :], r["eq"][:, :], ALU.add))
            vec.tensor_copy(idx_i[:, :], idx_f[:, :]).then_inc(picked, 1)
            link(vec.tensor_scalar(sc1["mx"][:, :], top[:, 0:1], 1.0, None, ALU.mult))
            vec.tensor_scalar(top[:, :], top[:, :], sc1["mx"][:, 0:1], None, ALU.subtract).then_inc(exp_in, 1)
            dve.wait_ge(exp_out, 3)
            link(vec.tensor_reduce(sc1["sm"][:, :], wts[:, :], AX.X, ALU.add))
            link(vec.reciprocal(sc1["rc"][:, :], sc1["sm"][:, :]))
            vec.tensor_scalar(wts[:, :], wts[:, :], sc1["rc"][:, 0:1], None, ALU.mult).then_inc(weighted, 1)
            dve.wait_ge(spread, 1)
            link(vec.tensor_copy(wb[:, :], ps[3][:, 0:2]))
            dve.wait_ge(big, 16 * 8)
            for k in range(2):
                link(vec.tensor_scalar(w2[:, k, :, :], w2[:, k, :, :], wb[:, k:k + 1], None, ALU.mult))
                link(vec.tensor_scalar(b2[:, k, :], b2[:, k, :], wb[:, k:k + 1], None, ALU.mult))
            link(vec.tensor_tensor(b2[:, 0, :], b2[:, 0, :], b2[:, 1, :], ALU.add))
            vec.memset(sc1["mx"][:, :], 0.0).then_inc(gelud, 2)
            vec.memset(sc1["sm"][:, :], 0.0).then_inc(evac, 2)
            vec.memset(sc1["rc"][:, :], 0.0).then_inc(scaled, 1)
            per = 4 * GB
            with dve.Fori(0, NG) as i:
                m = [0]

                def done(ins):
                    m[0] += 1
                    ins.then_inc(fin, 1)

                for u in range(GB):
                    dve.wait_ge(o_ready, i * GB + (u + 1))
                    vec.tensor_tensor(nv[:, u, :], ps[6 + u % 2][:, 0:D], b2[:, 0, :], ALU.add).then_inc(evac, 1)
                for u in range(GB):
                    dve.wait_ge(evac, i * GB + (u + 3))
                    done(vec.tensor_tensor(nv[:, u, :], nv[:, u, :], xn[:, ds(i * GB + u, 1), :], ALU.add))
                dve.wait_ge(fin, i * per + GB)
                own_wait(dve, g)
                layer_norm_group(dve, nc, g, lambda u: nv[:, u, :], lambda u: nv[:, u, :], t2, i * LN_STEPS, i)
                dve.wait_ge(t2["step"], i * LN_STEPS + LN_STEPS)
                for u in range(GB):
                    done(vec.tensor_tensor(nv[:, u, :], nv[:, u, :], gam[:, :], ALU.mult))
                dve.wait_ge(fin, i * per + 2 * GB)
                for u in range(GB):
                    done(vec.tensor_tensor(nv[:, u, :], nv[:, u, :], bet[:, :], ALU.add))
                dve.wait_ge(fin, i * per + 3 * GB)
                for u in range(GB):
                    done(vec.tensor_tensor(g["X"][:, ds(i * GB + u, 1), :], g["X"][:, ds(i * GB + u, 1), :], nv[:, u, :], ALU.add))
                dve.wait_ge(fin, i * per + per)

def stage_heads(nc, sb, sem, g):
    t = norm_tiles(sb, sem, "ln3")
    xn, xt = sb("wh_xn", [P, GB, D]), sb("wh_xt", [P, 2, GN])
    w = sb("wh_w", [P, 2, D])
    bias, a_src, a_dst = (sb("wh_" + k, [P, D]) for k in ("bias", "asrc", "adst"))
    wh, prod = sb("wh_out", [P, GB, HEADS, HD + 1]), sb("wh_prod", [P, 2, D])
    ad = sb("wh_ad", [P, NB, HEADS])
    loaded, trans, copied, whole, step, stored, ad_stored, evac = (sem("wh_" + n) for n in (
        "loaded", "trans", "copied", "whole", "step", "stored", "ad_stored", "evac"))
    ps = g["ps"]
    with nc.Block() as block:
        @block.sync
        def _(sp):
            sp.dma_start(w[:, :, :], g["L1_gnn_W_T"].rearrange("(c p) d -> p c d", p=P)).then_inc(loaded, 16)
            for tile, name in ((bias, "L1_gnn_b"), (a_src, "L1_gnn_a_src"), (a_dst, "L1_gnn_a_dst")):
                sp.dma_start(tile[:, :], g[name].to_broadcast([P, D])).then_inc(loaded, 16)
            with sp.Fori(0, NG) as i:
                sp.wait_ge(evac, i * GB + 2 * GB)
                sp.dma_start(g["wh"][ds(i * GN, GN), :].rearrange("(u p) d -> p u d", p=P), wh[:, :, :, :].rearrange("p u h d -> p u (h d)")).then_inc(stored, 16)
            sp.wait_ge(step, NB * 4)
            sp.dma_start(g["ad"].rearrange("(b p) h -> p b h", p=P), ad[:, :, :]).then_inc(ad_stored, 16)
            sp.wait_ge(ad_stored, 16)
            sp.wait_ge(stored, 16 * NG)

        @block.tensor
        def _(pe):
            pe.wait_ge(loaded, 64)
            with pe.Fori(0, NG) as i:
                pe.wait_ge(t["step"], i * LN_STEPS + LN_STEPS)
                transpose_group(pe, nc, xn, g["ident"], ps, trans)
                pe.wait_ge(copied, i * 4 + 4)
                for u in range(GB):
                    pe.wait_ge(evac, i * GB + (GB + u - 3))
                    for c in range(2):
                        m = nc.tensor.matmul(ps[4 + u % 4][:, 0:D], xt[:, c, u * P:(u + 1) * P], w[:, c, :], start=c == 0, stop=c == 1)
                    m.then_inc(whole, 1)
                pe.wait_ge(evac, i * GB + 2 * GB)

        @block.scalar
        def _(act):
            with act.Fori(0, NG) as i:
                root_group(act, nc, t, i * LN_STEPS)
                copy_transposed(act, nc, ps, xt, trans, i * (2 * GB), copied)

        @block.vector
        def _(dve):
            vec = nc.vector
            vec.memset(g["AS"][:, NB:NB + 1, :], 0.0).then_inc(evac, GB - 1)
            vec.memset(wh[:, :, :, HD:HD + 1], 1.0).then_inc(evac, 1)
            dve.wait_ge(evac, GB)
            dve.wait_ge(loaded, 64)
            with dve.Fori(0, NG) as i:
                layer_norm_group(dve, nc, g, lambda u: g["X"][:, ds(i * GB + u, 1), :], lambda u: xn[:, u, :], t, i * LN_STEPS, i)
                for u in range(GB):
                    dve.wait_ge(whole, i * GB + (u + 1))
                    vec.tensor_tensor(wh[:, u, :, 0:HD], ps[4 + u % 4][:, 0:D].rearrange("p (h d) -> p h d", h=HEADS),
                                      bias[:, :].rearrange("p (h d) -> p h d", h=HEADS), ALU.add).then_inc(evac, 1)
                for u in range(GB):
                    dve.wait_ge(evac, i * GB + (GB + u + 1))
                    for k, a in ((0, a_src), (1, a_dst)):
                        vec.tensor_tensor(prod[:, k, :].rearrange("p (h d) -> p h d", h=HEADS), wh[:, u, :, 0:HD],
                                          a[:, :].rearrange("p (h d) -> p h d", h=HEADS), ALU.mult).then_inc(step, 1)
                    for k in range(2):
                        dve.wait_ge(step, i * (4 * GB) + (4 * u + k + 1))
                        out = g["AS"][:, ds(i * GB + u, 1), 0:HEADS] if k == 0 else ad[:, ds(i * GB + u, 1), :]
                        vec.tensor_reduce(out.rearrange("p a h -> p (a h)"), prod[:, k, :].rearrange("p (h d) -> p h d", h=HEADS),
                                          AX.X, ALU.add).then_inc(step, 1)
                    dve.wait_ge(step, i * (4 * GB) + 4 * (u + 1))
                dve.wait_ge(stored, i * 16 + 16)


def stage_maxima(nc, sb, sem, g):
    idx = sb("mx_idx", [P, 2, HU], I32)
    adr = sb("mx_rows", [P, U, HEADS])
    pick = sb("mx_pick", [P, U, P])
    pen = sb("mx_pen", [P, U, P], BF16)
    diag = sb("mx_diag", [P, U, HEADS, P])
    ident4 = sb("mx_ident4", [P, HEADS, P], BF16)
    best = sb("mx_best", [P, UP, HEADS])
    mx = sb("mx_table", [P, NB + 1, HEADS])
    free = sb("mx_free", [1, 2])
    staged, kept, picked, crossed, penned, diag_v, summed, reduced, stepped, consts = (sem("mx_" + n) for n in (
        "staged", "kept", "picked", "crossed", "penned", "diag_v", "summed", "reduced", "stepped", "consts"))
    ps = g["ps"]
    got0 = 16 * GU * TURNS
    VH = 1
    NBK = 4
    with nc.Block() as block:
        @block.gpsimd
        def _(pool):
            pool.memset(free[:, 0:1], 0.0).then_inc(summed, UP)
            gather_rows(pool, nc, g, g["ad"], adr, idx, staged, summed)

        @block.scalar
        def _(act):
            for h in range(2):
                stage_indices(nc, g, idx, 0, h, staged)
            act.wait_ge(consts, 3)
            with act.Fori(0, TURNS) as i:
                for q in range(GPT):
                    u0 = q * GU
                    act.wait_ge(g["got"][q], i * (16 * GU) + (got0 + 16 * GU))
                    if q % 2 == 1:
                        stage_indices(nc, g, idx, i + 1, q // 2, staged)
                    nc.scalar.copy(g["ADE"][:, ds(i * U + u0, GU), :], adr[:, u0:u0 + GU, :]).then_inc(kept, 1)
                    act.wait_ge(summed, i * UP + 2 * (q + 1))
                    for u in range(u0, u0 + GU):
                        for k in range(VH, HEADS):
                            m = nc.scalar.activation(diag[:, u, k, :], g["ident"][:, :], ACT.Copy, scale=adr[:, u, k:k + 1])
                    m.then_inc(crossed, 1)
                    act.wait_ge(picked, i * GPT + (q + 1))
                    nc.scalar.activation(pen[:, u0:u0 + GU, :].rearrange("p u s -> p (u s)"), pick[:, u0:u0 + GU, :].rearrange("p u s -> p (u s)"),
                                         ACT.Copy, scale=BIG, bias=-BIG).then_inc(penned, 1)

        @block.tensor
        def _(pe):
            pe.wait_ge(consts, 3)
            with pe.Fori(0, TURNS) as i:
                for k in range(UP):
                    pe.wait_ge(reduced, i * UP + (k + 1))
                    if k % 2 == 0:
                        pe.wait_ge(penned, i * GPT + (k // 2 + 1))
                    for u in (2 * k, 2 * k + 1):
                        nc.tensor.matmul(ps[u % 8][:, :], pen[:, u, :], ident4[:, :, :].rearrange("p h e -> p (h e)"), start=True, stop=False)
                    if k % 2 == 0:
                        pe.wait_ge(diag_v, i * GPT + (k // 2 + 1))
                        pe.wait_ge(crossed, i * GPT + (k // 2 + 1))
                    for u in (2 * k, 2 * k + 1):
                        m = nc.tensor.matmul(ps[u % 8][:, :], pick[:, u, :], diag[:, u, :, :].rearrange("p h e -> p (h e)"),
                                             start=False, stop=True)
                    m.then_inc(summed, 1)

        @block.vector
        def _(dve):
            vec = nc.vector
            vec.memset(mx[:, :, :], -BIG).then_inc(consts, 1)
            for k in range(HEADS):
                c = vec.tensor_copy(ident4[:, k, :], g["ident"][:, :])
            c.then_inc(consts, 1)
            vec.memset(free[:, 1:2], 0.0).then_inc(reduced, NBK)
            vec.memset(g["ADE"][:, NI:NI + U, :], 0.0).then_inc(consts, 1)
            dve.wait_ge(consts, 3)

            def prepare(i, q):
                u0 = q * GU
                dve.wait_ge(summed, i * UP + 2 * (q + 1))
                one_hots(nc, g, pick, i, u0, GU).then_inc(picked, 1)
                dve.wait_ge(g["got"][q], i * (16 * GU) + (got0 + 16 * GU))
                vec.tensor_tensor(diag[:, u0:u0 + GU, 0:VH, :],
                                  g["ident"][:, :].rearrange("p (a b e) -> p a b e", a=1, b=1).to_broadcast([P, GU, VH, P]),
                                  adr[:, u0:u0 + GU, 0:VH].rearrange("p u (h a) -> p u h a", a=1).to_broadcast([P, GU, VH, P]), ALU.mult).then_inc(diag_v, 1)

            def reduce(i, k):
                dve.wait_ge(summed, i * UP + (UP + k + 1))
                vec.tensor_reduce(best[:, k, :], g["banks"][:, 2 * k % 8:2 * k % 8 + 2, :].rearrange("p u (h e) -> p h u e", h=HEADS), AX.XY, ALU.max).then_inc(reduced, 1)

            def merge(i, k, b):
                dve.wait_ge(reduced, i * UP + (NBK + k + 1))
                dve.wait_ge(stepped, i * UP + (k + 1))
                mb = mx[:, ds(b, 1), :].rearrange("p a h -> p (a h)")
                vec.tensor_tensor(mb, mb, best[:, k, :], ALU.max).then_inc(stepped, 1)

            def finish(i, q, blocks):
                reduce(i, 2 * q)
                reduce(i, 2 * q + 1)
                merge(i, 2 * q, blocks[0])
                merge(i, 2 * q + 1, blocks[1])

            vec.memset(free[:, 1:2], 0.0).then_inc(stepped, 1)
            prepare(0, 0)
            with dve.Fori(0, TURNS - 1) as i:
                blocks = pair_blocks(nc, g, mybir.EngineType.DVE, i, 0, UP)
                for q in range(GPT):
                    prepare(*((i, q + 1) if q < GPT - 1 else (i + 1, 0)))
                    finish(i, q, blocks[2 * q:2 * q + 2])
            blocks = pair_blocks(nc, g, mybir.EngineType.DVE, TURNS - 1, 0, UP)
            for q in range(GPT):
                if q < GPT - 1:
                    prepare(TURNS - 1, q + 1)
                finish(TURNS - 1, q, blocks[2 * q:2 * q + 2])
            dve.wait_ge(stepped, NI // 2 + 1)
            vec.tensor_tensor(mx[:, :, :], mx[:, :, :], g["AS"][:, :, 0:HEADS], ALU.add).then_inc(stepped, 1)
            dve.wait_ge(stepped, NI // 2 + 2)
            vec.scalar_tensor_tensor(out=g["AS"][:, :, HEADS:2 * HEADS], in0=mx[:, :, :], scalar=0.2, in1=mx[:, :, :],
                                     op0=ALU.mult, op1=ALU.max).then_inc(stepped, 1)


def stage_attend(nc, sb, sem, g):
    W = D + HEADS
    idx = sb("at_idx", [P, 2, HU], I32)
    rows = sb("at_rows", [P, U, W])
    pick = sb("at_pick", [P, U, P])
    pick_t = sb("at_pick_t", [P, HU, P])
    ex = sb("at_ex", [P, 2, HU, HEADS])
    z = sb("at_z", [P, 2, HU, HEADS])
    msg = sb("at_msg", [P, HU, W])
    free = sb("at_free", [1, 1])
    staged, picked, turned, tcopied, ea_done, soft, exped, messaged, summed, added = (sem("at_" + n) for n in (
        "staged", "picked", "turned", "tcopied", "ea_done", "soft", "exped", "messaged", "summed", "added"))
    ps = g["ps"]
    tp = [ps[0], ps[1]]
    ea = [ps[2], ps[3]]
    HP = UP // 2
    sums = [ps[4 + k] for k in range(HP)]
    got0 = 2 * 16 * GU * TURNS

    def after(i, h):
        return (i, 1) if h == 0 else (i + 1, 0)

    with nc.Block() as block:
        @block.gpsimd
        def _(pool):
            pool.memset(free[:, 0:1], 0.0).then_inc(summed, UP)
            gather_rows(pool, nc, g, g["wh"], rows, idx, staged, summed)

        @block.scalar
        def _(act):
            def turn(i, h):
                for q in range(2):
                    act.wait_ge(turned, i * 4 + (2 * h + q + 1))
                    nc.scalar.copy(pick_t[:, 4 * q:4 * q + 4, :].rearrange("p u e -> p (u e)"), tp[q][:, :]).then_inc(tcopied, 1)

            def exponentials(i, h):
                act.wait_ge(soft, i * 8 + (4 * h + 4))
                nc.scalar.activation(ex[:, h, :, :], z[:, h, :, :], ACT.Exp).then_inc(exped, 1)

            for h in range(2):
                stage_indices(nc, g, idx, 0, h, staged)
            turn(0, 0)
            exponentials(0, 0)
            with act.Fori(0, TURNS) as i:
                for h in range(2):
                    turn(*after(i, h))
                    for q in (2 * h, 2 * h + 1):
                        act.wait_ge(g["got"][q], i * (16 * GU) + (got0 + 16 * GU))
                    stage_indices(nc, g, idx, i + 1, h, staged)
                    exponentials(*after(i, h))

        @block.tensor
        def _(pe):
            def turns(i, h, q):
                pe.wait_ge(picked, i * GPT + (2 * h + q + 1))
                for k in range(GU):
                    m = nc.tensor.transpose(tp[q][:, k * P:(k + 1) * P], pick[:, h * HU + q * GU + k, :], g["ident"][:, :])
                m.then_inc(turned, 1)

            def scores(i, h):
                blocks = pair_blocks(nc, g, mybir.EngineType.PE, i, h * HP, HP)
                for q in range(2):
                    pe.wait_ge(tcopied, i * 4 + (2 * h + q + 1))
                    for u in range(GU * q, GU * q + GU):
                        m = nc.tensor.matmul(ea[h][:, u * 2 * HEADS:(u + 1) * 2 * HEADS], pick_t[:, u, :],
                                             g["AS"][:, ds(blocks[u // 2], 1), :].rearrange("p a h -> p (a h)"), start=True, stop=True)
                m.then_inc(ea_done, 1)

            turns(0, 0, 0)
            turns(0, 0, 1)
            scores(0, 0)
            turns(0, 1, 0)
            with pe.Fori(0, TURNS) as i:
                for h in range(2):
                    for k in range(HP):
                        n = h * HP + k
                        if k % 2 == 0:
                            pe.wait_ge(messaged, i * GPT + (n // 2 + 1))
                        pe.wait_ge(added, i * UP + (n + 1))
                        for u in (2 * k, 2 * k + 1):
                            m = nc.tensor.matmul(sums[k][:, 0:W], pick[:, h * HU + u, :], msg[:, u, :], start=u == 2 * k, stop=u == 2 * k + 1)
                        m.then_inc(summed, 1)
                        if k == 0:
                            turns(*after(i, h), 1)
                        if k == 1:
                            scores(*after(i, h))
                    turns(i + 1, h, 0)

        @block.vector
        def _(dve):
            vec = nc.vector

            def picks(i, q):
                one_hots(nc, g, pick, i, q * GU, GU).then_inc(picked, 1)

            def softmax(i, h):
                e = ea[h][:, 0:HU * 2 * HEADS].rearrange("p (u k) -> p u k", u=HU)
                zz = z[:, h, :, :]
                dve.wait_ge(ea_done, i * 2 + (h + 1))
                vec.tensor_tensor(zz, e[:, :, 0:HEADS], g["ADE"][:, ds(i * U + h * HU, HU), :], ALU.add).then_inc(soft, 1)
                dve.wait_ge(soft, i * 8 + (4 * h + 1))
                vec.scalar_tensor_tensor(out=zz, in0=zz, scalar=0.2, in1=zz, op0=ALU.mult, op1=ALU.max).then_inc(soft, 1)
                dve.wait_ge(soft, i * 8 + (4 * h + 2))
                vec.tensor_tensor(zz, zz, e[:, :, HEADS:2 * HEADS], ALU.subtract).then_inc(soft, 1)
                dve.wait_ge(soft, i * 8 + (4 * h + 3))
                vec.tensor_scalar(zz, zz, 0.0, None, ALU.min).then_inc(soft, 1)

            def messages(i, h, q):
                dve.wait_ge(exped, i * 2 + (h + 1))
                dve.wait_ge(g["got"][2 * h + q], i * (16 * GU) + (got0 + 16 * GU))
                vec.tensor_tensor(msg[:, q * GU:(q + 1) * GU, :].rearrange("p u (h d) -> p (u h) d", h=HEADS),
                                  rows[:, h * HU + q * GU:h * HU + (q + 1) * GU, :].rearrange("p u (h d) -> p (u h) d", h=HEADS),
                                  ex[:, h, q * GU:(q + 1) * GU, :].rearrange("p u (h a) -> p (u h) a", a=1).to_broadcast([P, GU * HEADS, HD + 1]),
                                  ALU.mult).then_inc(messaged, 1)

            def adds(i, h, q, blocks):
                for k in (2 * q, 2 * q + 1):
                    n = h * HP + k
                    dve.wait_ge(summed, i * UP + (UP + n + 1))
                    dve.wait_ge(added, i * UP + (n + HP))
                    acc = g["NUM"][:, ds(blocks[k], 1), :].rearrange("p a n -> p (a n)")
                    vec.tensor_tensor(acc, acc, sums[k][:, 0:W], ALU.add).then_inc(added, 1)

            def half(i, h, last=False):
                blocks = pair_blocks(nc, g, mybir.EngineType.DVE, i, h * HP, HP)
                adds(i, h, 0, blocks)
                softmax(*after(i, h))
                for q in range(2):
                    if q == 1:
                        adds(i, h, 1, blocks)
                    picks(i + 1, 2 * h + q)
                    if not last:
                        messages(*after(i, h), q)

            vec.memset(g["NUM"][:, :, :], 0.0).then_inc(added, HP)
            for q in range(GPT):
                picks(0, q)
            softmax(0, 0)
            messages(0, 0, 0)
            messages(0, 0, 1)
            with dve.Fori(0, TURNS - 1) as i:
                half(i, 0)
                half(i, 1)
            half(TURNS - 1, 0)
            half(TURNS - 1, 1, last=True)


def stage_project(nc, sb, sem, g):
    t = norm_tiles(sb, sem, "ln4")
    xn, xt = sb("xp_xn", [P, GB, D]), sb("xp_xt", [P, 2, GN])
    w = sb("xp_w", [P, 2, 4 * D])
    b_ih, b_hh = sb("xp_bih", [P, 4 * D]), sb("xp_bhh", [P, 4 * D])
    out = sb("xp_out", [P, GB, 4 * D])
    den, att = sb("xp_den", [P, NB, HEADS]), sb("xp_att", [P, GB, D])
    loaded, trans, copied, whole, evac, step, stored, scaled = (sem("xp_" + n) for n in (
        "loaded", "trans", "copied", "whole", "evac", "step", "stored", "scaled"))
    ps = g["ps"]
    Q = 2 * GB
    with nc.Block() as block:
        @block.sync
        def _(sp):
            sp.dma_start(w[:, :, :], g["L1_ffn_W_ihT"].rearrange("(c p) n -> p c n", p=P)).then_inc(loaded, 16)
            sp.dma_start(b_ih[:, :], g["L1_ffn_b_ihP"].to_broadcast([P, 4 * D])).then_inc(loaded, 16)
            sp.dma_start(b_hh[:, :], g["L1_ffn_b_hhP"].to_broadcast([P, 4 * D])).then_inc(loaded, 16)
            with sp.Fori(0, NG) as i:
                sp.wait_ge(evac, i * Q + (Q + 4))
                sp.dma_start(g["xp"][ds(i * GN, GN), :].rearrange("(u p) n -> p u n", p=P), out[:, :, :]).then_inc(stored, 16)
            sp.wait_ge(stored, 16 * NG)

        @block.tensor
        def _(pe):
            pe.wait_ge(scaled, 6)
            with pe.Fori(0, NG) as i:
                pe.wait_ge(t["step"], i * LN_STEPS + LN_STEPS)
                transpose_group(pe, nc, xn, g["ident"], ps, trans)
                pe.wait_ge(copied, i * 4 + 4)
                for q in range(Q):
                    u, n = q // 2, q % 2
                    pe.wait_ge(evac, i * Q + (q + 1))
                    for c in range(2):
                        m = nc.tensor.matmul(ps[4 + q % 4][:, :], xt[:, c, u * P:(u + 1) * P], w[:, c, n * 512:(n + 1) * 512], start=c == 0, stop=c == 1)
                    m.then_inc(whole, 1)
                pe.wait_ge(evac, i * Q + (Q + 4))

        @block.scalar
        def _(act):
            with act.Fori(0, NG) as i:
                root_group(act, nc, t, i * LN_STEPS)
                copy_transposed(act, nc, ps, xt, trans, i * (2 * GB), copied)

        @block.vector
        def _(dve):
            vec = nc.vector
            vec.memset(out[:, 0, 0:1], 0.0).then_inc(evac, 4)
            dve.wait_ge(evac, 4)
            dve.wait_ge(loaded, 48)
            vec.tensor_tensor(b_ih[:, :], b_ih[:, :], b_hh[:, :], ALU.add).then_inc(step, 1)
            dve.wait_ge(step, 1)
            for row in (w[:, 0, :], w[:, 1, :], b_ih[:, :]):
                for a, b in ((0, 2 * HD), (3 * HD, 4 * HD)):
                    v = row.rearrange("p (j k) -> p j k", j=4)[:, :, a:b]
                    vec.tensor_scalar(v, v, 0.5, None, ALU.mult).then_inc(scaled, 1)
            dve.wait_ge(scaled, 6)
            dn = g["NUM"][:, 0:NB, HD:D + HEADS:HD + 1]
            vec.tensor_scalar(den[:, :, :], dn, 0.0, None, ALU.is_equal).then_inc(step, 1)
            dve.wait_ge(step, 2)
            vec.tensor_tensor(den[:, :, :], den[:, :, :], dn, ALU.add).then_inc(step, 1)
            dve.wait_ge(step, 3)
            vec.reciprocal(den[:, :, :], den[:, :, :]).then_inc(step, 1)
            dve.wait_ge(step, 4)
            per = 2 * GB
            with dve.Fori(0, NG) as i:
                for u in range(GB):
                    vec.tensor_tensor(att[:, u, :].rearrange("p (h d) -> p h d", h=HEADS),
                                      g["NUM"][:, ds(i * GB + u, 1), :].rearrange("p a (h d) -> p (a h) d", h=HEADS)[:, :, 0:HD],
                                      den[:, ds(i * GB + u, 1), :].rearrange("p a h -> p h a").to_broadcast([P, HEADS, HD]), ALU.mult).then_inc(step, 1)
                dve.wait_ge(step, i * per + (4 + GB))
                for u in range(GB):
                    xb = g["X"][:, ds(i * GB + u, 1), :].rearrange("p a d -> p (a d)")
                    vec.tensor_tensor(xb, xb, att[:, u, :], ALU.add).then_inc(step, 1)
                dve.wait_ge(step, i * per + (4 + 2 * GB))
                own_wait(dve, g)
                layer_norm_group(dve, nc, g, lambda u: g["X"][:, ds(i * GB + u, 1), :], lambda u: xn[:, u, :], t, i * LN_STEPS, i)
                for q in range(Q):
                    dve.wait_ge(whole, i * Q + (q + 1))
                    vec.tensor_tensor(out[:, q // 2, (q % 2) * 512:(q % 2 + 1) * 512], ps[4 + q % 4][:, :],
                                      b_ih[:, (q % 2) * 512:(q % 2 + 1) * 512], ALU.add).then_inc(evac, 1)
                dve.wait_ge(stored, i * 16 + 16)


def stage_lstm(nc, sb, sem, g):
    w = sb("ls_w", [P, 2, 4, D])
    xp = sb("ls_xp", [P, 2, 4 * D])
    s = sb("ls_s", [P, 4 * HD])
    o = sb("ls_o", [P, HD])
    ab = sb("ls_ab", [P, 2 * HD])
    ht = sb("ls_ht", [P, LU, HD])
    free = sb("ls_free", [P, 1])
    ps = g["ps"]
    tc, h = ps[4][:, 0:HD], ps[5][:, 0:HD]
    A = 3 * HD
    w_loaded, zeroed, gates_ready, gates_done, ab_ready, c_ready, tc_ready, h_made, h_ready, kept, xp_used = (sem("ls_" + n) for n in (
        "w_loaded", "zeroed", "gates_ready", "gates_done", "ab_ready", "c_ready", "tc_ready", "h_made", "h_ready", "kept", "xp_used"))
    xp_in = [sem("ls_xp0"), sem("ls_xp1")]
    PER = 2 * LU
    KN = LU // KU
    with nc.Block() as block:
        @block.sync
        def _(sp):
            sp.dma_start(w[:, :, :, :].rearrange("p c j n -> p c (j n)"), g["L1_ffn_W_hhT"]).then_inc(w_loaded, 16)
            sp.wait_ge(zeroed, 1)
            for b in range(2):
                sp.dma_start(xp[0:LU, b, :], g["xp"][b * LU:(b + 1) * LU, :]).then_inc(xp_in[b], 16)
            with sp.Fori(0, N // PER - 1) as i:
                for b in range(2):
                    sp.wait_ge(xp_used, i * 2 + (b + 1))
                    sp.dma_start(xp[0:LU, b, :], g["xp"][ds((i * 2 + (b + 2)) * LU, LU), :]).then_inc(xp_in[b], 16)

        @block.gpsimd
        def _(pool):
            pool.memset(free[:, :], 0.0).then_inc(kept, KN)
            with pool.Fori(0, N // LU) as i:
                for q in range(KN):
                    pool.wait_ge(h_ready, i * LU + (KU * (q + 1) + 1))
                    nc.gpsimd.tensor_copy(g["HIST"][:, :, ds(i * LU + KU * q, KU)],
                                          ht[:, KU * q:KU * (q + 1), 0:33:32].rearrange("p u c -> p c u")).then_inc(kept, 1)

        @block.tensor
        def _(pe):
            pe.wait_ge(zeroed, 4)
            with pe.Fori(0, N // PER) as i:
                for b in range(2):
                    pe.wait_ge(xp_in[b], i * 16 + 16)
                    for u in range(LU):
                        k = b * LU + u
                        parts = ((ps[k % 2], 0, A), (ps[2 + k % 2], A, D))
                        for bank, lo, hi in parts:
                            for j in range(4):
                                m = nc.tensor.matmul(bank[32 * j:32 * j + 32, 0:hi - lo], g["ident"][:, u:u + 1].to_broadcast([P, 32]),
                                                     xp[:, b, j * D + lo:j * D + hi], start=True, stop=False, tile_position=(0, 32 * j))
                        if u == LU - 1:
                            m.then_inc(xp_used, 1)
                        pe.wait_ge(h_ready, i * PER + (k + 1))
                        for bank, lo, hi in parts:
                            for c in range(2):
                                for j in range(4):
                                    m = nc.tensor.matmul(bank[32 * j:32 * j + 32, 0:hi - lo], ht[:, (u - 1) % LU, 32 * c:32 * c + 32],
                                                         w[:, c, j, lo:hi], start=False, stop=c == 1, tile_position=(0, 32 * j))
                            m.then_inc(gates_ready, 1)

        @block.scalar
        def _(act):
            with act.Fori(0, N // PER) as i:
                for k in range(PER):
                    act.wait_ge(gates_ready, i * (2 * PER) + (2 * k + 1))
                    nc.scalar.activation(s[:, 0:A], ps[k % 2][:, 0:A], ACT.Tanh).then_inc(gates_done, 1)
                    act.wait_ge(gates_ready, i * (2 * PER) + (2 * k + 2))
                    nc.scalar.activation(o[:, :], ps[2 + k % 2][:, 0:HD], ACT.Tanh)
                    act.wait_ge(c_ready, i * PER + (k + 2))
                    nc.scalar.activation(tc, s[:, A:4 * HD], ACT.Tanh, scale=0.5).then_inc(tc_ready, 1)

        @block.vector
        def _(dve):
            vec = nc.vector
            vec.memset(xp[:, :, :], 0.0).then_inc(zeroed, 1)
            vec.memset(ht[:, :, :], 0.0).then_inc(h_ready, 1)
            vec.memset(s[:, A:4 * HD], 0.0).then_inc(c_ready, 1)
            dve.wait_ge(w_loaded, 16)
            for lo, hi, scale in ((0, 2 * HD, 0.25), (2 * HD, A, 0.5), (A, D, 0.25)):
                v = w[:, :, :, lo:hi].rearrange("p c j n -> p (c j) n")
                vec.tensor_scalar(v, v, scale, None, ALU.mult).then_inc(zeroed, 1)
            dve.wait_ge(c_ready, 1)
            dve.wait_ge(h_ready, 1)
            with dve.Fori(0, N // PER) as i:
                for k in range(PER):
                    n1, n2, u = i * PER + (k + 1), i * PER + (k + 2), k % LU
                    dve.wait_ge(gates_done, n1)
                    vec.scalar_tensor_tensor(out=ab[:, :], in0=s[:, 0:2 * HD], scalar=1.0, in1=s[:, 2 * HD:4 * HD],
                                             op0=ALU.add, op1=ALU.mult).then_inc(ab_ready, 1)
                    dve.wait_ge(ab_ready, n1)
                    vec.scalar_tensor_tensor(out=s[:, A:4 * HD], in0=ab[:, HD:2 * HD], scalar=0.5, in1=ab[:, 0:HD],
                                             op0=ALU.mult, op1=ALU.add).then_inc(c_ready, 1)
                    dve.wait_ge(tc_ready, n1)
                    vec.scalar_tensor_tensor(out=h, in0=o[:, :], scalar=1.0, in1=tc,
                                             op0=ALU.add, op1=ALU.mult).then_inc(h_made, 1)
                    dve.wait_ge(h_made, n1)
                    if u % KU == 0:
                        dve.wait_ge(kept, i * (2 * KN) + (k // KU + 1))
                    vec.transpose(ht[:, u, :], h).then_inc(h_ready, 1)


def stage_finish(nc, sb, sem, g):
    wl = sb("fi_wl", [P, 2, 2])
    bl = sb("fi_bl", [P, 2])
    fw, bw, nbw = sb("fi_fw", [P, 2]), sb("fi_bw", [P, 2]), sb("fi_nbw", [P, 2])
    gate = sb("fi_gate", [P, N])
    l0 = sb("fi_l0", [P, 2, 512])
    inc = sb("fi_inc", [P, N])
    tmp = sb("fi_tmp", [P, N])
    loaded, ready, logits, compared, step, turned, added, stored = (sem("fi_" + n) for n in (
        "loaded", "ready", "logits", "compared", "step", "turned", "added", "stored"))
    ps = g["ps"]
    hist = g["HIST"]
    chunks = [(a, min(512, N - a)) for a in range(0, N, 512)]
    with nc.Block() as block:
        @block.sync
        def _(sp):
            sp.dma_start(wl[:, :, :], g["L1_ffn_W_linT"]).then_inc(loaded, 16)
            sp.dma_start(bl[:, :], g["L1_ffn_b_lin"].to_broadcast([P, 2])).then_inc(loaded, 16)
            sp.dma_start(fw[:, :], g["L1_ffn_fw_attT"]).then_inc(loaded, 16)
            sp.dma_start(bw[:, :], g["L1_ffn_bw_attT"]).then_inc(loaded, 16)
            for q in range(NG):
                sp.wait_ge(added, min(NB, (q + 1) * GB))
                a, b = q * GB, min((q + 1) * GB, NB - 1)
                sp.dma_start(g["out"][a * P:b * P, :].rearrange("(b p) d -> p b d", p=P), g["X"][:, a:b, :]).then_inc(stored, 16)
            sp.dma_start(g["out"][(NB - 1) * P:N, :], g["X"][0:TAIL, NB - 1, :]).then_inc(stored, 16)
            sp.wait_ge(stored, 16 * (NG + 1))

        @block.tensor
        def _(pe):
            pe.wait_ge(ready, 3)
            for q, (a, n) in enumerate(chunks):
                if q >= 2:
                    pe.wait_ge(compared, 2 * (q - 1))
                for l in range(2):
                    for c in range(2):
                        m = nc.tensor.matmul(ps[2 * (q % 2) + l][:, 0:n], wl[:, c, l:l + 1].to_broadcast([P, P]), hist[:, c, a:a + n],
                                             start=c == 0, stop=c == 1)
                m.then_inc(logits, 1)
            pe.wait_ge(step, 2 * 6)
            for b in range(NB):
                rows = P if b < NB - 1 else TAIL
                if b >= 4:
                    pe.wait_ge(added, b - 3)
                for c in range(2):
                    m = nc.tensor.transpose(ps[4 + b % 4][0:rows, c * P:(c + 1) * P], hist[:, c, b * P:b * P + rows], g["ident"][:, :])
                m.then_inc(turned, 1)

        @block.vector
        def _(dve):
            vec = nc.vector
            n = [0]

            def link(ins):
                n[0] += 1
                ins.then_inc(step, 1)
                dve.wait_ge(step, n[0])

            dve.wait_ge(loaded, 64)
            vec.tensor_scalar(wl[:, :, :], wl[:, :, :], 0.5, None, ALU.mult).then_inc(ready, 1)
            vec.tensor_scalar(nbw[:, :], bw[:, :], -1.0, None, ALU.mult).then_inc(ready, 1)
            vec.memset(tmp[:, 0:1], 0.0).then_inc(ready, 1)
            dve.wait_ge(ready, 3)
            for q, (a, m) in enumerate(chunks):
                dve.wait_ge(logits, q + 1)
                if q >= 2:
                    dve.wait_ge(compared, 2 * (q - 1))
                vec.tensor_scalar(l0[:, q % 2, 0:m], ps[2 * (q % 2)][:, 0:m], bl[:, 0:1], None, ALU.add).then_inc(compared, 1)
                dve.wait_ge(compared, 2 * q + 1)
                vec.scalar_tensor_tensor(out=gate[:, a:a + m], in0=ps[2 * (q % 2) + 1][:, 0:m], scalar=bl[:, 1:2], in1=l0[:, q % 2, 0:m],
                                         op0=ALU.add, op1=ALU.is_gt).then_inc(compared, 1)
            dve.wait_ge(compared, 2 * len(chunks))
            for c in range(2):
                h = hist[:, c, :]
                link(vec.scalar_tensor_tensor(out=tmp[:, :], in0=h, scalar=0.5, in1=gate[:, :], op0=ALU.mult, op1=ALU.mult))
                link(vec.tensor_tensor_scan(inc[:, :], tmp[:, :], tmp[:, :], 0.0, ALU.add, ALU.bypass))
                link(vec.tensor_tensor(tmp[:, :], inc[:, :], tmp[:, :], ALU.subtract))
                link(vec.scalar_tensor_tensor(out=h, in0=tmp[:, :], scalar=fw[:, c:c + 1], in1=h, op0=ALU.mult, op1=ALU.add))
                link(vec.tensor_scalar(tmp[:, :], inc[:, :], inc[:, N - 1:N], None, ALU.subtract))
                link(vec.scalar_tensor_tensor(out=h, in0=tmp[:, :], scalar=nbw[:, c:c + 1], in1=h, op0=ALU.mult, op1=ALU.add))
            for b in range(NB):
                rows = P if b < NB - 1 else TAIL
                dve.wait_ge(turned, b + 1)
                x = g["X"][0:rows, b, :].rearrange("p (j c n) -> p c j n", j=4, c=2)
                vec.tensor_tensor(x, x, ps[4 + b % 4][0:rows, 0:D].rearrange("p (c j n) -> p c j n", c=2, j=4), ALU.add).then_inc(added, 1)


_INS = ["x", "src", "dst", "edge_weight", "L0_ffn_Wr", "L0_ffn_br", "L0_ffn_W1", "L0_ffn_b1T", "L0_ffn_W2", "L0_ffn_b2",
        "L0_ffn_gamma", "L0_ffn_beta", "L1_gnn_W_T", "L1_gnn_b", "L1_gnn_a_src", "L1_gnn_a_dst", "L1_ffn_W_ihT",
        "L1_ffn_W_hhT", "L1_ffn_b_ihP", "L1_ffn_b_hhP", "L1_ffn_W_linT", "L1_ffn_b_lin", "L1_ffn_fw_attT", "L1_ffn_bw_attT"]


def gate_order(w):
    import numpy as np
    w = np.asarray(w).reshape(4, 4, D // 4, -1)
    return np.ascontiguousarray(w.transpose(1, 0, 2, 3).reshape(4 * D, -1))


def unit_order(w):
    import numpy as np
    w = np.asarray(w)
    w = w.reshape(4, 2, 32, -1).transpose(0, 2, 1, 3).reshape(P, 2, -1)
    return np.ascontiguousarray(w)


def lay_out(i):
    import numpy as np
    i = {k: np.asarray(v) for k, v in i.items()}
    o = {k: i[k] for k in _INS if k in i}
    o["L0_ffn_b1T"] = np.ascontiguousarray(i["L0_ffn_b1"].reshape(NEXP, FC, P).transpose(2, 0, 1))
    o["L1_gnn_W_T"] = np.ascontiguousarray(i["L1_gnn_W"].T)
    o["L1_ffn_W_ihT"] = np.ascontiguousarray(gate_order(i["L1_ffn_W_ih"]).T)
    o["L1_ffn_W_hhT"] = unit_order(gate_order(i["L1_ffn_W_hh"]).T)
    o["L1_ffn_b_ihP"] = gate_order(i["L1_ffn_b_ih"]).reshape(1, -1)
    o["L1_ffn_b_hhP"] = gate_order(i["L1_ffn_b_hh"]).reshape(1, -1)
    o["L1_ffn_W_linT"] = unit_order(i["L1_ffn_W_lin"].T)
    o["L1_ffn_fw_attT"] = unit_order(i["L1_ffn_fw_att"].T).reshape(P, 2)
    o["L1_ffn_bw_attT"] = unit_order(i["L1_ffn_bw_att"].T).reshape(P, 2)
    o["L1_gnn_a_src"] = i["L1_gnn_a_src"].reshape(1, D)
    o["L1_gnn_a_dst"] = i["L1_gnn_a_dst"].reshape(1, D)
    o["L1_gnn_b"] = i["L1_gnn_b"].reshape(1, D)
    o["L1_ffn_b_lin"] = i["L1_ffn_b_lin"].reshape(1, 2)
    return o


def build(nc, ins, out):
    with ExitStack() as ctx:
        g = dict(ins)
        sem = lambda name: ctx.enter_context(nc.semaphore(name))
        keep = lambda name, shape, dt=F32: ctx.enter_context(nc.sbuf_tensor(name, shape, dt))
        g["banks"] = ctx.enter_context(nc.psum_tensor("banks", [P, 8, 512], F32))
        g["ps"] = [g["banks"][:, k, :] for k in range(8)]
        g["y"] = nc.dram_tensor("y_table", (NP, D), F32, kind="Internal").ap()
        g["rec"] = [nc.dram_tensor(f"rec_table{k}", (P * NI, RF), F32, kind="Internal").ap() for k in range(WAYS)]
        g["wh"] = nc.dram_tensor("wh_table", (NP, D + HEADS), F32, kind="Internal").ap()
        g["ad"] = nc.dram_tensor("alpha_dst_table", (NP, HEADS), F32, kind="Internal").ap()
        g["xp"] = nc.dram_tensor("projections", (NP, 4 * D), F32, kind="Internal").ap()
        g["out"] = out
        g["waits_carried"] = {e: sem("waits_carried_" + e) for e in ("DVE", "Pool")}
        g["started"] = sem("started")
        g["scattered"] = [sem(f"scattered{k}") for k in range(WAYS)]
        g["got"] = [sem(f"got{q}") for q in range(GPT)]
        g["ident"] = keep("ident", [P, P])
        g["iota"] = keep("iota", [P, P])
        g["X"] = keep("X", [P, NB + 1, D])

        def stage(f):
            with ExitStack() as own:
                f(nc, lambda name, shape, dt=F32: own.enter_context(nc.sbuf_tensor(name, shape, dt)), sem, g)

        stage(stage_normalise)
        with ExitStack() as items:
            kept = lambda name, shape, dt=F32: items.enter_context(nc.sbuf_tensor(name, shape, dt))
            g["BW"] = kept("item_block", [P, NI])
            g["BI"] = kept("pair_block", [1, NI // 2 + UP], I32)
            with ExitStack() as recs:
                g["REC"] = recs.enter_context(nc.sbuf_tensor("records", [EP, EC, RF], F32))
                g["POS"] = recs.enter_context(nc.sbuf_tensor("places", [EP, EC], I32))
                stage(stage_places)
                stage(stage_scatter)
            g["DST"] = kept("item_dst", [P, NI + U], I32)
            g["LO"] = kept("item_lo", [P, NI + U])
            g["EW"] = kept("item_weight", [P, NI + U])
            stage(stage_items)
            stage(stage_aggregate)
            stage(stage_experts)
            g["AS"] = kept("alpha_src_and_max", [P, NB + 1, 2 * HEADS])
            stage(stage_heads)
            g["NUM"] = kept("numerators", [P, NB + 1, D + HEADS])
            with ExitStack() as scores:
                g["ADE"] = scores.enter_context(nc.sbuf_tensor("item_alpha_dst", [P, NI + U, HEADS], F32))
                stage(stage_maxima)
                stage(stage_attend)
            stage(stage_project)
        g["HIST"] = keep("history", [P, 2, N])
        stage(stage_lstm)
        stage(stage_finish)


def kernel(**inputs):
    from concourse import bacc
    from concourse.bass_utils import run_bass_kernel_spmd

    nc = bacc.Bacc("TRN2", target_bir_lowering=False, num_devices=1)
    arrays = lay_out(inputs)
    aps = {k: nc.dram_tensor("in_" + k, a.shape, mybir.dt.from_np(a.dtype), kind="ExternalInput").ap() for k, a in arrays.items()}
    out = nc.dram_tensor("out", (N, D), F32, kind="ExternalOutput").ap()
    build(nc, aps, out)
    r = run_bass_kernel_spmd(nc, [{"in_" + k: a for k, a in arrays.items()}], core_ids=[0])
    return r.results[0]["out"]
```
